# Optimizing a Trainium2 kernel written in Bass

```python
import numpy as np
import jax
import jax.numpy as jnp

def _softmax(x, axis=-1):
    return jax.nn.softmax(x, axis=axis)

def _gelu(x):
    return jax.nn.gelu(x, approximate=True)

def _silu(x):
    return jax.nn.silu(x)

def _sigmoid(x):
    return jax.nn.sigmoid(x)

def _layernorm(x, axis=-1, eps=1e-05):
    m = jnp.mean(x, axis=axis, keepdims=True)
    v = jnp.var(x, axis=axis, keepdims=True)
    return (x - m) / jnp.sqrt(v + eps)

def _scatter_add(tgt, idx, src, axis=0):
    return tgt.at[idx].add(src)

def _segment_sum(src, seg, n):
    return jax.ops.segment_sum(src, seg, n)
kernel_name = 'mk_perceiver_d1_seqx_r4_20a85d'

def setup_inputs(seed: int=0):
    np.random.seed(seed)
    _w = jnp.asarray

    def _rec_inputs():
        import jax
        import jax.numpy as jnp
        _rk = jax.random.key(seed)
        x = -0.0005146 + 1 * jax.random.normal(jax.random.fold_in(_rk, 1), (8, 64, 256), jnp.float32)
        _lenS = 64 - jax.random.randint(jax.random.fold_in(_rk, 7), (8,), 0, max(1, 64 // 4) + 1, jnp.int32)
        _lenS2 = 1601 - jax.random.randint(jax.random.fold_in(_rk, 8), (8,), 0, max(1, 1601 // 4) + 1, jnp.int32)
        _ctx_768P = jax.random.normal(jax.random.fold_in(_rk, 11), (8, 16, 192), jnp.float32)
        _ctx_768c = jax.random.dirichlet(jax.random.fold_in(_rk, 511), 0.3 * jnp.ones((16,), jnp.float32), (8, 1601))
        _ctx_768t = jnp.einsum('bsk,bkd->bsd', _ctx_768c, _ctx_768P)
        _ctx_768t = _ctx_768t * jax.lax.rsqrt(jnp.mean(jnp.square(_ctx_768t)) + 1e-12) * 0.953939
        ctx_768 = -0.00040386 + 0.999972 * (_ctx_768t + 0.3 * jax.random.normal(jax.random.fold_in(_rk, 611), (8, 1601, 192), jnp.float32))
        _validS = jnp.arange(64)[None, :] < _lenS[:, None]
        _validS2 = jnp.arange(1601)[None, :] < _lenS2[:, None]
        _causal = jnp.tril(jnp.ones((64, 64), dtype=bool))
        mask_BxS2_bk0 = jnp.logical_not(jnp.broadcast_to(_validS2[:, :], (8, 1601)))
        return (x, ctx_768, mask_BxS2_bk0)
    x, ctx_768, mask_BxS2_bk0 = _rec_inputs()

    def _L0_xattn_setup():
        import jax, jax.numpy as jnp
        import numpy as np
        DIM_IN, DIM_LAT, DIM_HEAD = (192, 256, 64)
        INNER = max(DIM_LAT, DIM_IN)
        HEADS = INNER // DIM_HEAD
        SCALE = DIM_HEAD ** (-0.5)
        RMS_EPS = 1e-08
        LN_EPS = 1e-05

        def layernorm(x, g, b):
            mu = jnp.mean(x, axis=-1, keepdims=True)
            var = jnp.mean((x - mu) ** 2, axis=-1, keepdims=True)
            return (x - mu) * jax.lax.rsqrt(var + LN_EPS) * g + b

        def rmsnorm(x, gamma):
            norm = jnp.sqrt(jnp.sum(x * x, axis=-1, keepdims=True)) * x.shape[-1] ** (-0.5)
            return x / jnp.maximum(norm, RMS_EPS) * gamma
        key = jax.random.key(seed)
        ks = jax.random.split(key, 12)
        b, n, m = (4, 1024, 128)
        x = jax.random.normal(ks[0], (b, n, DIM_IN), jnp.float32)
        latents = jax.random.normal(ks[1], (b, m, DIM_LAT), jnp.float32)
        mask = jax.random.randint(ks[2], (b, n), 0, 2).astype(bool)
        s = lambda k, sh, fan: jax.random.normal(k, sh, jnp.float32) * fan ** (-0.5)
        return {'x': x, 'latents': latents, 'mask': mask, 'ln_x_g': jnp.ones((DIM_IN,), jnp.float32), 'ln_x_b': jnp.zeros((DIM_IN,), jnp.float32), 'ln_l_g': jnp.ones((DIM_LAT,), jnp.float32), 'ln_l_b': jnp.zeros((DIM_LAT,), jnp.float32), 'qn_g': jnp.ones((DIM_HEAD,), jnp.float32), 'kn_g': jnp.ones((DIM_HEAD,), jnp.float32), 'Wq': s(ks[3], (INNER, DIM_LAT), DIM_LAT), 'Wkv': s(ks[4], (2 * INNER, DIM_IN), DIM_IN), 'Wlkv': s(ks[5], (2 * INNER, DIM_LAT), DIM_LAT), 'Wo': s(ks[6], (DIM_LAT, INNER), INNER), 'bo': jnp.zeros((DIM_LAT,), jnp.float32)}
    _L0_xattn_all = _L0_xattn_setup()
    _L0_xattn_in = {k: v for k, v in _L0_xattn_all.items() if k in ('ln_x_g', 'ln_x_b', 'ln_l_g', 'ln_l_b', 'qn_g', 'kn_g', 'Wq', 'Wkv', 'Wlkv', 'Wo', 'bo')}
    del _L0_xattn_all

    def _L0_attn_setup():
        import jax, jax.numpy as jnp
        import numpy as np
        B, T, HID = (4, 512, 256)
        NH = 4
        KD, VD = (128, 256)
        DK, DV = (KD // NH, VD // NH)
        R = 32
        GLR = 64
        EPS = 1e-05

        def _rwkv6_scan(r, k, v, w, u):

            def step(S, xs):
                r_t, k_t, v_t, w_t = xs
                kv = k_t[..., :, None] * v_t[..., None, :]
                o_t = jnp.einsum('bhk,bhkv->bhv', r_t, S + u[None, :, :, None] * kv)
                S = jnp.exp(w_t)[..., None] * S + kv
                return (S, o_t)
            S0 = jnp.zeros(r.shape[:2] + (r.shape[-1], v.shape[-1]), r.dtype)
            mv = lambda x: jnp.moveaxis(x, 2, 0)
            _, o = jax.lax.scan(step, S0, (mv(r), mv(k), mv(v), mv(w)))
            return jnp.moveaxis(o, 0, 2)
        key = jax.random.key(seed)
        ks = jax.random.split(key, 20)
        g = lambda i, shape, s=0.02: jax.random.normal(ks[i], shape, dtype=jnp.float32) * s
        return {'hidden_states': jax.random.normal(ks[0], (B, T, HID), dtype=jnp.float32), 'mu0': g(1, (HID,), 0.1), 'W_x0': g(2, (5 * R, HID)), 'W_x2': g(3, (HID, 5 * R)), 'x_bias': g(4, (5, HID), 0.1), 'W_r': g(5, (KD, HID)), 'W_w1': g(6, (GLR, HID)), 'W_w2': g(7, (KD, GLR)), 'b_w2': g(8, (KD,), 0.1), 'W_k': g(9, (KD, HID)), 'W_v': g(10, (VD, HID)), 'W_g': g(11, (VD, HID)), 'bonus': g(12, (NH, DK), 0.1), 'gn_weight': jnp.ones((VD,), jnp.float32) + g(13, (VD,), 0.05), 'gn_bias': g(14, (VD,), 0.05), 'W_o': g(15, (HID, VD))}
    _L0_attn_all = _L0_attn_setup()
    _L0_attn_in = {k: v for k, v in _L0_attn_all.items() if k in ('mu0', 'W_x0', 'W_x2', 'x_bias', 'W_r', 'W_w1', 'W_w2', 'b_w2', 'W_k', 'W_v', 'W_g', 'bonus', 'gn_weight', 'gn_bias', 'W_o')}
    del _L0_attn_all

    def _L0_ffn_setup():
        import jax, jax.numpy as jnp
        import numpy as np
        HIDDEN = 256
        INTER = 128
        N_EXPERTS = 16
        N_GROUP = 4
        TOPK_GROUP = 2
        TOP_K = 4
        SCALING = 2.5

        def _gate(x_flat, gate_w, e_bias):
            logits = x_flat @ gate_w.T
            scores = jax.nn.sigmoid(logits)
            scores_for_choice = scores + e_bias[None, :]
            T = x_flat.shape[0]
            per_group = N_EXPERTS // N_GROUP
            grouped = scores_for_choice.reshape(T, N_GROUP, per_group)
            top2, _ = jax.lax.top_k(grouped, 2)
            group_scores = top2.sum(-1)
            _, group_idx = jax.lax.top_k(group_scores, TOPK_GROUP)
            group_mask = jax.nn.one_hot(group_idx, N_GROUP, dtype=jnp.float32).sum(1) > 0
            score_mask = jnp.repeat(group_mask, per_group, axis=-1)
            tmp_scores = jnp.where(score_mask, scores_for_choice, 0.0)
            _, topk_idx = jax.lax.top_k(tmp_scores, TOP_K)
            topk_weight = jnp.take_along_axis(scores, topk_idx, axis=1)
            topk_weight = topk_weight / (topk_weight.sum(-1, keepdims=True) + 1e-20)
            topk_weight = topk_weight * SCALING
            return (topk_idx, topk_weight)
        key = jax.random.key(seed)
        ks = jax.random.split(key, 8)
        B, S = (2, 512)
        hidden_states = jax.random.normal(ks[0], (B, S, HIDDEN), dtype=jnp.float32)
        gate_w = jax.random.normal(ks[1], (N_EXPERTS, HIDDEN), dtype=jnp.float32) * 0.02
        e_bias = jnp.zeros((N_EXPERTS,), dtype=jnp.float32)
        gate_proj = jax.random.normal(ks[2], (N_EXPERTS, INTER, HIDDEN), dtype=jnp.float32) * 0.02
        up_proj = jax.random.normal(ks[3], (N_EXPERTS, INTER, HIDDEN), dtype=jnp.float32) * 0.02
        down_proj = jax.random.normal(ks[4], (N_EXPERTS, HIDDEN, INTER), dtype=jnp.float32) * 0.02
        shared_gate_w = jax.random.normal(ks[5], (INTER, HIDDEN), dtype=jnp.float32) * 0.02
        shared_up_w = jax.random.normal(ks[6], (INTER, HIDDEN), dtype=jnp.float32) * 0.02
        shared_down_w = jax.random.normal(ks[7], (HIDDEN, INTER), dtype=jnp.float32) * 0.02
        return {'hidden_states': hidden_states, 'gate_w': gate_w, 'e_bias': e_bias, 'gate_proj': gate_proj, 'up_proj': up_proj, 'down_proj': down_proj, 'shared_gate_w': shared_gate_w, 'shared_up_w': shared_up_w, 'shared_down_w': shared_down_w}
    _L0_ffn_all = _L0_ffn_setup()
    _L0_ffn_in = {k: v for k, v in _L0_ffn_all.items() if k in ('gate_w', 'e_bias', 'gate_proj', 'up_proj', 'down_proj', 'shared_gate_w', 'shared_up_w', 'shared_down_w')}
    del _L0_ffn_all
    return {'x': x, 'ctx_768': ctx_768, 'mask_BxS2_bk0': mask_BxS2_bk0, 'L0_xattn_ln_x_g': _L0_xattn_in['ln_x_g'], 'L0_xattn_ln_x_b': _L0_xattn_in['ln_x_b'], 'L0_xattn_ln_l_g': _L0_xattn_in['ln_l_g'], 'L0_xattn_ln_l_b': _L0_xattn_in['ln_l_b'], 'L0_xattn_qn_g': _L0_xattn_in['qn_g'], 'L0_xattn_kn_g': _L0_xattn_in['kn_g'], 'L0_xattn_Wq': _L0_xattn_in['Wq'], 'L0_xattn_Wkv': _L0_xattn_in['Wkv'], 'L0_xattn_Wlkv': _L0_xattn_in['Wlkv'], 'L0_xattn_Wo': _L0_xattn_in['Wo'], 'L0_xattn_bo': _L0_xattn_in['bo'], 'L0_attn_mu0': _L0_attn_in['mu0'], 'L0_attn_W_x0': _L0_attn_in['W_x0'], 'L0_attn_W_x2': _L0_attn_in['W_x2'], 'L0_attn_x_bias': _L0_attn_in['x_bias'], 'L0_attn_W_r': _L0_attn_in['W_r'], 'L0_attn_W_w1': _L0_attn_in['W_w1'], 'L0_attn_W_w2': _L0_attn_in['W_w2'], 'L0_attn_b_w2': _L0_attn_in['b_w2'], 'L0_attn_W_k': _L0_attn_in['W_k'], 'L0_attn_W_v': _L0_attn_in['W_v'], 'L0_attn_W_g': _L0_attn_in['W_g'], 'L0_attn_bonus': _L0_attn_in['bonus'], 'L0_attn_gn_weight': _L0_attn_in['gn_weight'], 'L0_attn_gn_bias': _L0_attn_in['gn_bias'], 'L0_attn_W_o': _L0_attn_in['W_o'], 'L0_ffn_gate_w': _L0_ffn_in['gate_w'], 'L0_ffn_e_bias': _L0_ffn_in['e_bias'], 'L0_ffn_gate_proj': _L0_ffn_in['gate_proj'], 'L0_ffn_up_proj': _L0_ffn_in['up_proj'], 'L0_ffn_down_proj': _L0_ffn_in['down_proj'], 'L0_ffn_shared_gate_w': _L0_ffn_in['shared_gate_w'], 'L0_ffn_shared_up_w': _L0_ffn_in['shared_up_w'], 'L0_ffn_shared_down_w': _L0_ffn_in['shared_down_w']}

def reference(x, ctx_768, mask_BxS2_bk0, L0_xattn_ln_x_g, L0_xattn_ln_x_b, L0_xattn_ln_l_g, L0_xattn_ln_l_b, L0_xattn_qn_g, L0_xattn_kn_g, L0_xattn_Wq, L0_xattn_Wkv, L0_xattn_Wlkv, L0_xattn_Wo, L0_xattn_bo, L0_attn_mu0, L0_attn_W_x0, L0_attn_W_x2, L0_attn_x_bias, L0_attn_W_r, L0_attn_W_w1, L0_attn_W_w2, L0_attn_b_w2, L0_attn_W_k, L0_attn_W_v, L0_attn_W_g, L0_attn_bonus, L0_attn_gn_weight, L0_attn_gn_bias, L0_attn_W_o, L0_ffn_gate_w, L0_ffn_e_bias, L0_ffn_gate_proj, L0_ffn_up_proj, L0_ffn_down_proj, L0_ffn_shared_gate_w, L0_ffn_shared_up_w, L0_ffn_shared_down_w):
    import jax
    import jax.numpy as jnp

    def _L0_xattn_ref(x, latents, mask, ln_x_g, ln_x_b, ln_l_g, ln_l_b, qn_g, kn_g, Wq, Wkv, Wlkv, Wo, bo):
        import jax, jax.numpy as jnp
        import numpy as np
        DIM_IN, DIM_LAT, DIM_HEAD = (192, 256, 64)
        INNER = max(DIM_LAT, DIM_IN)
        HEADS = INNER // DIM_HEAD
        SCALE = DIM_HEAD ** (-0.5)
        RMS_EPS = 1e-08
        LN_EPS = 1e-05

        def layernorm(x, g, b):
            mu = jnp.mean(x, axis=-1, keepdims=True)
            var = jnp.mean((x - mu) ** 2, axis=-1, keepdims=True)
            return (x - mu) * jax.lax.rsqrt(var + LN_EPS) * g + b

        def rmsnorm(x, gamma):
            norm = jnp.sqrt(jnp.sum(x * x, axis=-1, keepdims=True)) * x.shape[-1] ** (-0.5)
            return x / jnp.maximum(norm, RMS_EPS) * gamma
        b, n, _ = x.shape
        m = latents.shape[1]
        xn = layernorm(x, ln_x_g, ln_x_b)
        ln = layernorm(latents, ln_l_g, ln_l_b)
        q = ln @ Wq.T
        kv = jnp.concatenate([xn @ Wkv.T, ln @ Wlkv.T], axis=1)
        k, v = (kv[..., :INNER], kv[..., INNER:])
        split_heads = lambda t: t.reshape(t.shape[0], t.shape[1], HEADS, DIM_HEAD).transpose(0, 2, 1, 3)
        q, k, v = (split_heads(q), split_heads(k), split_heads(v))
        qn = rmsnorm(q, qn_g) * SCALE
        kn = rmsnorm(k, kn_g)
        attn = jnp.einsum('bhid,bhjd->bhij', qn, kn)
        full_mask = jnp.pad(mask, ((0, 0), (0, m)), constant_values=True)
        attn = jnp.where(full_mask[:, None, None, :], attn, -jnp.finfo(attn.dtype).max)
        attn = jax.nn.softmax(attn, axis=-1)
        out = jnp.einsum('bhij,bhjd->bhid', attn, v)
        out = out.transpose(0, 2, 1, 3).reshape(b, m, INNER)
        return out @ Wo.T + bo

    def _L0_attn_ref(hidden_states, mu0, W_x0, W_x2, x_bias, W_r, W_w1, W_w2, b_w2, W_k, W_v, W_g, bonus, gn_weight, gn_bias, W_o):
        import jax, jax.numpy as jnp
        import numpy as np
        B, T, HID = (4, 512, 256)
        NH = 4
        KD, VD = (128, 256)
        DK, DV = (KD // NH, VD // NH)
        R = 32
        GLR = 64
        EPS = 1e-05

        def _rwkv6_scan(r, k, v, w, u):

            def step(S, xs):
                r_t, k_t, v_t, w_t = xs
                kv = k_t[..., :, None] * v_t[..., None, :]
                o_t = jnp.einsum('bhk,bhkv->bhv', r_t, S + u[None, :, :, None] * kv)
                S = jnp.exp(w_t)[..., None] * S + kv
                return (S, o_t)
            S0 = jnp.zeros(r.shape[:2] + (r.shape[-1], v.shape[-1]), r.dtype)
            mv = lambda x: jnp.moveaxis(x, 2, 0)
            _, o = jax.lax.scan(step, S0, (mv(r), mv(k), mv(v), mv(w)))
            return jnp.moveaxis(o, 0, 2)
        x = hidden_states
        shifted = jnp.pad(x, ((0, 0), (1, 0), (0, 0)))[:, :-1]
        delta = shifted - x
        xp = jnp.tanh((x + delta * mu0) @ W_x0.T)
        xp = xp.reshape(x.shape[0], x.shape[1], 5, R)
        mus = jnp.einsum('blnr,hnr->blnh', xp, W_x2.reshape(HID, 5, R)) + x_bias
        mu_r, mu_w, mu_k, mu_v, mu_g = (mus[:, :, i] for i in range(5))
        r = (x + delta * mu_r) @ W_r.T
        w = jnp.tanh((x + delta * mu_w) @ W_w1.T) @ W_w2.T + b_w2
        k = (x + delta * mu_k) @ W_k.T
        v = (x + delta * mu_v) @ W_v.T
        g = (x + delta * mu_g) @ W_g.T
        split = lambda t, d: t.reshape(t.shape[0], t.shape[1], NH, d).transpose(0, 2, 1, 3)
        r_, k_, w_ = (split(r, DK), split(k, DK), split(w, DK))
        v_ = split(v, DV)
        w_ = -jnp.exp(w_)
        o = _rwkv6_scan(r_, k_, v_, w_, bonus)
        o = o.transpose(0, 2, 1, 3)
        mean = o.mean(-1, keepdims=True)
        var = o.var(-1, keepdims=True)
        o = (o - mean) * jax.lax.rsqrt(var + EPS)
        o = o.reshape(x.shape[0], x.shape[1], VD) * gn_weight + gn_bias
        o = o * jax.nn.silu(g)
        return o @ W_o.T

    def _L0_ffn_ref(hidden_states, gate_w, e_bias, gate_proj, up_proj, down_proj, shared_gate_w, shared_up_w, shared_down_w):
        import jax, jax.numpy as jnp
        import numpy as np
        HIDDEN = 256
        INTER = 128
        N_EXPERTS = 16
        N_GROUP = 4
        TOPK_GROUP = 2
        TOP_K = 4
        SCALING = 2.5

        def _gate(x_flat, gate_w, e_bias):
            logits = x_flat @ gate_w.T
            scores = jax.nn.sigmoid(logits)
            scores_for_choice = scores + e_bias[None, :]
            T = x_flat.shape[0]
            per_group = N_EXPERTS // N_GROUP
            grouped = scores_for_choice.reshape(T, N_GROUP, per_group)
            top2, _ = jax.lax.top_k(grouped, 2)
            group_scores = top2.sum(-1)
            _, group_idx = jax.lax.top_k(group_scores, TOPK_GROUP)
            group_mask = jax.nn.one_hot(group_idx, N_GROUP, dtype=jnp.float32).sum(1) > 0
            score_mask = jnp.repeat(group_mask, per_group, axis=-1)
            tmp_scores = jnp.where(score_mask, scores_for_choice, 0.0)
            _, topk_idx = jax.lax.top_k(tmp_scores, TOP_K)
            topk_weight = jnp.take_along_axis(scores, topk_idx, axis=1)
            topk_weight = topk_weight / (topk_weight.sum(-1, keepdims=True) + 1e-20)
            topk_weight = topk_weight * SCALING
            return (topk_idx, topk_weight)
        B, S, H = hidden_states.shape
        x = hidden_states.reshape(-1, H)
        T = x.shape[0]
        topk_idx, topk_weight = _gate(x, gate_w, e_bias)
        g = jnp.einsum('th,eih->eti', x, gate_proj)
        u = jnp.einsum('th,eih->eti', x, up_proj)
        inter = jax.nn.silu(g) * u
        expert_out = jnp.einsum('eti,ehi->eth', inter, down_proj)
        sel = expert_out[topk_idx, jnp.arange(T)[:, None]]
        y = jnp.einsum('tkh,tk->th', sel, topk_weight)
        y = y.reshape(B, S, H)
        sg = hidden_states @ shared_gate_w.T
        su = hidden_states @ shared_up_w.T
        shared_out = jax.nn.silu(sg) * su @ shared_down_w.T
        return y + shared_out
    x = x + _L0_xattn_ref(ctx_768, _layernorm(x, axis=-1), mask_BxS2_bk0, L0_xattn_ln_x_g, L0_xattn_ln_x_b, L0_xattn_ln_l_g, L0_xattn_ln_l_b, L0_xattn_qn_g, L0_xattn_kn_g, L0_xattn_Wq, L0_xattn_Wkv, L0_xattn_Wlkv, L0_xattn_Wo, L0_xattn_bo)
    x = x + _L0_attn_ref(_layernorm(x, axis=-1), L0_attn_mu0, L0_attn_W_x0, L0_attn_W_x2, L0_attn_x_bias, L0_attn_W_r, L0_attn_W_w1, L0_attn_W_w2, L0_attn_b_w2, L0_attn_W_k, L0_attn_W_v, L0_attn_W_g, L0_attn_bonus, L0_attn_gn_weight, L0_attn_gn_bias, L0_attn_W_o)
    x = x + _L0_ffn_ref(_layernorm(x, axis=-1), L0_ffn_gate_w, L0_ffn_e_bias, L0_ffn_gate_proj, L0_ffn_up_proj, L0_ffn_down_proj, L0_ffn_shared_gate_w, L0_ffn_shared_up_w, L0_ffn_shared_down_w)
    return x

_drawn_inputs = setup_inputs


def setup_inputs(seed=0):
    import zlib

    import numpy as np

    out = dict(_drawn_inputs(seed))
    spreads = {'L0_xattn_ln_x_g': (1.0, 0.2),
     'L0_xattn_ln_x_b': (0.0, 0.1),
     'L0_xattn_ln_l_g': (1.0, 0.2),
     'L0_xattn_ln_l_b': (0.0, 0.269),
     'L0_xattn_qn_g': (1.0, 0.555),
     'L0_xattn_kn_g': (1.0, 0.59),
     'L0_xattn_bo': (0.0, 0.1),
     'L0_ffn_e_bias': (0.0, 0.527)}
    factors = {'L0_attn_mu0': 8.0,
     'L0_attn_W_x0': 8.0,
     'L0_attn_W_x2': 8.0,
     'L0_attn_x_bias': 3.46,
     'L0_attn_W_w1': 8.0,
     'L0_attn_W_w2': 8.0,
     'L0_attn_b_w2': 8.0,
     'L0_attn_bonus': 5.837,
     'L0_attn_gn_weight': 8.0,
     'L0_attn_gn_bias': 8.0,
     'L0_ffn_gate_w': 8.0,
     'L0_ffn_gate_proj': 4.157,
     'L0_ffn_up_proj': 4.12,
     'L0_ffn_down_proj': 4.105,
     'L0_ffn_shared_gate_w': 5.283,
     'L0_ffn_shared_up_w': 5.22,
     'L0_ffn_shared_down_w': 5.24}
    for name, (base, spread) in spreads.items():
        noise = np.random.default_rng([zlib.crc32(name.encode()), seed]).standard_normal(out[name].shape)
        drawn = base * np.exp(spread * noise) if base else spread * noise
        out[name] = jnp.asarray(drawn.astype(out[name].dtype))
    for name, factor in factors.items():
        out[name] = (out[name] * factor).astype(out[name].dtype)
    return out
```

```python
from contextlib import ExitStack

import numpy as np

import concourse.bass as bass
from concourse import mybir

F32 = mybir.dt.float32
F32R = mybir.dt.float32r
BF16 = mybir.dt.bfloat16
U8 = mybir.dt.uint8
I32 = mybir.dt.int32
ALU = mybir.AluOpType
ACT = mybir.ActivationFunctionType
AX = mybir.AxisListType

P = 128
B, T, D = 8, 64, 256
S, DC = 1601, 192
H, DH = 4, 64
NT = B * T // P
HALF = DC // 2
W = HALF + 1
ROW = 2 * W
MROW = 1680
MPIECE = B * MROW // P
LOWEST = -3e38
FULL = S // P
TAIL = S - FULL * P
NG = (FULL + 1) // 2 + 1
KEYS = S + T
NPAIR = H // 2
CH = 512
NCH = -(-KEYS // CH)
STEPS = NPAIR * NCH
NE, INTER, TOPK, TOPG, NGRP = 16, 128, 4, 2, 4
LEVELS = 6
LN_EPS = 1e-5
MASKED = -1e30
ARENA = 30574
NXH = 4


def constants():
    i = np.arange(P)
    same = i[:, None] // T == i[None, :] // T
    u, pos = i[:, None], i[None, :]
    sums = np.zeros((P, LEVELS, P), np.float32)
    pick = np.zeros((P, LEVELS, P // 2), np.int32)
    for lv in range(LEVELS):
        m = 1 << lv
        right = (pos // m) % 2 == 1
        sums[:, lv] = same & (u // m == pos // m) & np.where(right, u < pos, u > pos)
        queries = pos[:, right[0]]
        pick[:, lv] = (u // T == queries // T) & (u // (2 * m) == queries // (2 * m)) & ((u // m) % 2 == 0)
    e = np.arange(NE)
    return {
        "c_ident": np.eye(P, dtype=np.float32),
        "c_sums": sums,
        "c_pick": pick,
        "c_head": (i[:, None] // 32 == np.arange(4)[None, :]).astype(np.float32),
        "c_before": (e[None, :] < e[:, None]).astype(np.float32).reshape(1, NE * NE),
        "c_gbefore": (np.arange(4)[None, :] < np.arange(4)[:, None]).astype(np.float32).reshape(1, 16),
    }


def build(nc, a, out):
    x_dram = a["x"].rearrange("b t d -> (b t) d").rearrange("(i p) d -> p i d", p=P)
    out_dram = out.rearrange("b t d -> (b t) d").rearrange("(i p) d -> p i d", p=P)
    with ExitStack() as ctx:
        def sb(name, shape, dt=F32):
            return ctx.enter_context(nc.sbuf_tensor(name, shape, dt))

        def sem(name):
            return ctx.enter_context(nc.semaphore(name))

        ps = [ctx.enter_context(nc.psum_tensor(f"bank{i}", [P, 512], F32)) for i in range(8)]
        score_bank, k_bank, tx_bank, tp_bank, y_bank = ps[0:4], ps[4], ps[5], ps[6], ps[7]

        arena = sb("arena", [P, ARENA])

        def carve(at, *shapes):
            views = []
            for shape in shapes:
                n = int(np.prod(shape[1:]))
                v = arena[0:shape[0], at:at + n]
                if len(shape) == 3:
                    v = v.rearrange("p (a b) -> p a b", a=shape[1])
                if len(shape) == 4:
                    v = v.rearrange("p (a b c) -> p a b c", a=shape[1], b=shape[2])
                views.append(v)
                at += n
            assert at <= ARENA, at
            return (*views, at)

        ident = sb("ident", [P, P])
        sums = sb("sums", [P, LEVELS, P])
        pick = sb("pick", [P, LEVELS, P // 2], I32)
        headsel = sb("headsel", [P, 4])
        wkh = sb("wkh", [W, 2, D], F32R)
        wkl = sb("wkl", [W, 2, D], F32R)
        xhT = [sb(f"xhT{i}", [W, 2, 256], F32R) for i in range(2)]
        xhTl = [sb(f"xhTl{i}", [W, 2, 256], F32R) for i in range(2)]
        before = sb("before", [P, NE * NE])
        gbefore = sb("gbefore", [P, 16])
        neg_half = sb("neg_half", [P, 64])
        ones_row = sb("ones_row", [1, P])
        wkv = sb("wkv", [W, 2, 2 * D])
        lnx = sb("lnx", [HALF, 4])
        lnx_g, lnx_b = lnx[:, 0:2], lnx[:, 2:4]
        cols = sb("cols", [P, 19])
        lnl_g, lnl_b, mu0, bonus, qg, kg = (cols[:, i:j] for i, j in ((0, 2), (2, 4), (4, 6), (6, 7), (7, 8), (8, 9)))
        xbias = cols[:, 9:19].rearrange("p (c i) -> p c i", c=2)
        qkg = sb("qkg", [P, 1])
        wq = sb("wq", [P, 2, D])
        wlkv = sb("wlkv", [P, 2, 2 * D])
        wo = sb("wo", [P, 2, D])
        bo = sb("bo", [1, D])
        wx0 = sb("wx0", [P, 2, 160])
        wx2a = sb("wx2a", [P, D])
        wx2b = sb("wx2b", [32, D])
        wr = sb("wr", [P, 2, 128])
        wk = sb("wk", [P, 2, 128])
        ww1 = sb("ww1", [P, 2, 64])
        ww2 = sb("ww2", [65, 128])
        wv = sb("wv", [P, 2, D])
        wg = sb("wg", [P, 2, D])
        wo2 = sb("wo2", [P, 2, D])
        gnw = sb("gnw", [P, D])
        gnb = sb("gnb", [P, D])
        gatew = sb("gatew", [P, 2, NE])
        ebias = sb("ebias", [P, NE])
        mask_flat = sb("mask_flat", [P, MPIECE], BF16)
        mask_row = sb("mask_row", [P, 2, MROW], BF16)
        mask_bc = [sb(f"mask_bc{i}", [P, MROW], BF16) for i in range(2)]
        mask_in = mask_bc[1].bitcast(I32)[:, 0:MPIECE]

        X = sb("X", [P, NT, D])
        big = sb("big", [P, NT, D])
        st = sb("st", [P, NT, 6])
        mv = sb("mv", [P, NT, 2])
        rs = sb("rs", [P, NT])
        xT = sb("xT", [P, 2, B * T])
        qkss = sb("qkss", [P, 2 * NT * H])
        qkr = sb("qkr", [P, 2 * NT * H])
        oT = sb("oT", [P, NPAIR, B * T])
        oT2 = oT

        *xh, at = carve(0, *[(P, FULL + 1, ROW)] * NXH)
        at_kT1 = at + NPAIR * S
        *kT, at = carve(at, *[(P, NPAIR, S)] * 2)
        *pr, at = carve(at, *[(P, KEYS)] * 2)
        *pT, at = carve(at, *[(P, 4, P)] * 2)
        *kn, at = carve(at, *[(P, 512)] * 2)
        *kraw, at = carve(at, *[(P, 512)] * 2)
        xn, wkv_raw, _ = carve(at_kT1, (P, NT, D), (HALF, 2, 2 * D))
        ksq, qk, qb, klT, vlat, at = carve(at, (P, 512), (P, 2, NT, D), (P, B * NPAIR, P), (P, NPAIR, B * T), (T, B, D))
        cst = sb("cst", [P, 2, 2, 6])
        cmv = sb("cmv", [P, 2, 2, 2])
        crs = sb("crs", [P, 2, 2])
        kss = sb("kss", [P, 2, 8])
        kr = sb("kr", [P, 2, 8])
        mx = sb("mx", [P, 2, NCH])
        nm = sb("nm", [P, 2])
        ls = sb("ls", [P, 2, NCH])
        lsum = sb("lsum", [P, 2])
        rl = sb("rl", [P, 2])
        plat = sb("plat", [P, T])
        plT = sb("plT", [T, P])
        ysb = sb("ysb", [P, 2 * W])
        yT = sb("yT", [W, 2, P])

        eg, eu, ed, at = carve(0, (P, NE + 1, 2 * INTER), (P, NE + 1, 2 * INTER), (P, NE + 1, D))
        eg = eg.rearrange("p e (c i) -> p e c i", c=2)
        eu = eu.rearrange("p e (c i) -> p e c i", c=2)
        delta, at = carve(at, (P, 2, B * T))
        at_mixed = at
        *mixed, at_tmix = carve(at, *[(P, 2, B * T)] * 5)
        aT, _ = carve(at_mixed, (P, NT, H, P))
        sil0, sil1, inter0, inter1, at_pw = carve(at_mixed, *[(P, B * T)] * 4)
        sil, inter = [sil0, sil1], [inter0, inter1]
        pw, _ = carve(at_pw, (P, 2, NT * NE * NE))
        pw = [pw[:, k].rearrange("p (i a b) -> p i a b", i=NT, a=NE) for k in range(2)]
        *tmix, at = carve(at_tmix, *[(P, B * T)] * 2)
        xpa, rT, rkT, ew, vn, sg, sgb, ex, ruk, on, at = carve(
            at, (P, B * T), (P, B * T), (P, B * T), (P, NT, 128), (P, NT, D), (P, NT, D), (P, NT, D), (P, LEVELS, B * T),
            (P, B * T), (P, NT, D))
        acc = ex[:, 0:2, :].rearrange("p a (i d) -> p (a i) d", d=D)
        xpb = sb("xpb", [32, B * T])
        wt = sb("wt", [65, B * T])
        dcoef = sb("dcoef", [P, NT, 4])
        hs = sb("hs", [P, 4, NT * H])
        fe = sb("fe", [P, 12, NT, NE])
        fg = sb("fg", [P, 8, NT, NGRP])
        gw = sb("gw", [P, 3, NT, 16])

        x_in = sem("x_in"); ctx_first = sem("ctx_first"); lat_in = sem("lat_in"); setup_in = sem("setup_in"); mixer_in = sem("mixer_in"); expert_in = sem("expert_in")
        ctx_in = [sem(f"ctx_in{i}") for i in range(2)]; mask_in_sem = sem("mask_in_sem")
        stored = sem("stored")
        pool_const = sem("pool_const"); mask_ready = sem("mask_ready"); mask_rows = sem("mask_rows"); mask_spread = sem("mask_spread"); wk_split = sem("wk_split")
        ln_stats = sem("ln_stats"); ln_aggr = sem("ln_aggr"); ln_rstd = sem("ln_rstd"); ln_out = sem("ln_out")
        tok_T = sem("tok_T"); tok_T_evac = sem("tok_T_evac")
        wkv_bias = sem("wkv_bias"); wkv_ready = sem("wkv_ready")
        lat_mm = sem("lat_mm"); lat_evac = sem("lat_evac")
        vlat_mm = sem("vlat_mm"); vlat_evac = sem("vlat_evac")
        lat_sq = sem("lat_sq"); lat_ss = sem("lat_ss"); lat_r = sem("lat_r"); lat_n = sem("lat_n")
        lat_nT = sem("lat_nT"); lat_nT_evac = sem("lat_nT_evac");
        cstat = sem("cstat"); caggr = sem("caggr"); crstd = sem("crstd"); xh_ready = sem("xh_ready")
        xhT_mm = sem("xhT_mm"); xhT_evac = sem("xhT_evac"); xhT_low = sem("xhT_low")
        k_mm = sem("k_mm"); k_sq = sem("k_sq"); k_evac = sem("k_evac"); k_ss = sem("k_ss"); k_r = sem("k_r"); k_n = sem("k_n")
        kT_mm = sem("kT_mm"); kT_evac = sem("kT_evac")
        score_mm = sem("score_mm"); chunk_max = sem("chunk_max"); row_max = sem("row_max")
        exp_done = sem("exp_done"); row_sum = sem("row_sum"); row_inv = sem("row_inv"); plat_ready = sem("plat_ready")
        pT_mm = sem("pT_mm"); pT_evac = sem("pT_evac"); y_mm = sem("y_mm"); y_evac = sem("y_evac")
        yT_mm = sem("yT_mm"); yT_evac = sem("yT_evac"); o_mm = sem("o_mm"); o_evac = sem("o_evac")
        res_mm = sem("res_mm"); res_add = sem("res_add")
        d_ready = sem("d_ready"); xx_ready = sem("xx_ready"); xp_mm = sem("xp_mm"); xp_act = sem("xp_act")
        mu_mm = sem("mu_mm"); mu_use = sem("mu_use"); mixed_ready = sem("mixed_ready")
        r_mm = sem("r_mm"); r_evac = sem("r_evac"); kk_mm = sem("kk_mm"); kk_evac = sem("kk_evac")
        w1_mm = sem("w1_mm"); w1_act = sem("w1_act"); w2_mm = sem("w2_mm"); w2_act = sem("w2_act")
        v_mm = sem("v_mm"); v_evac = sem("v_evac"); g_mm = sem("g_mm"); g_act = sem("g_act")
        e_mm = sem("e_mm"); e_act = sem("e_act"); ruk_ready = sem("ruk_ready"); dc_mm = sem("dc_mm")
        level_ready = sem("level_ready"); a_zero = sem("a_zero"); a_mm = sem("a_mm"); a_pick = sem("a_pick")
        av_mm = sem("av_mm"); av_read = sem("av_read"); vec = sem("vec"); o_cent = sem("o_cent"); o_sq = sem("o_sq")
        gn_var = sem("gn_var"); gn_r = sem("gn_r"); gain_ready = sem("gain_ready"); o_gated = sem("o_gated"); oT2_mm = sem("oT2_mm"); oT2_evac = sem("oT2_evac")
        gate_mm = sem("gate_mm"); gate_exp = sem("gate_exp"); comb_ready = sem("comb_ready")
        gu_mm = sem("gu_mm"); silu = sem("silu"); inter_ready = sem("inter_ready"); down_mm = sem("down_mm"); acc_done = sem("acc_done")
        pool_tick = sem("pool_tick"); vec_tick = sem("vec_tick")

        def rows(t):
            return P if t < FULL else TAIL

        def tiles(g):
            return [2 * g, 2 * g + 1] if 2 * g + 1 < FULL else [2 * g]

        groups = B * NG
        chunks = B * STEPS
        steps = (B + 1) * (STEPS) + STEPS + 0

        def group_of(u):
            b, k = divmod(u, STEPS)
            return b * NG + k if b < B and k < NG else None

        def chunk_of(u):
            m = u - STEPS
            return m if 0 <= m < chunks else None

        def lag(u, n):
            return chunk_of(u - n) if u >= n else None

        def span(c):
            return c * CH, min(KEYS, (c + 1) * CH)

        def key_tiles(c):
            return [(t, t * P, t * P + rows(t)) for t in range(4 * c, min(4 * c + 4, FULL + 1))]

        block = ctx.enter_context(nc.Block())

        ORDER = [1, 0, 2, 3, 4]
        NORMS = [(0, NT), (0, NT), (0, 2), (2, 4), (0, 2), (2, 4)]

        def normed(n):
            return sum(hi - lo for lo, hi in NORMS[:n + 1])

        def kn_sq(i):
            return pr[i // 2][:, (i % 2) * 512:(i % 2 + 1) * 512]

        @block.sync
        def _(sp):
            for dst, src in (
                (ident[:], a["c_ident"]), (cols[:], a["v_cols"]), (lnx[:], a["v_lnx"]),
                (wkv_raw[:], a["t_Wkv"].rearrange("(c p) n -> p c n", p=HALF)),
            ):
                sp.dma_start(dst, src).then_inc(setup_in, 16)
            for b in range(B):
                if b >= 2:
                    sp.wait_ge(ctx_in[b % 2], 32 * (b // 2))
                if b >= NXH:
                    sp.wait_ge(y_mm, NPAIR * (b - NXH + 1))
                buf = xh[b % NXH]
                full = a["ctx_768"][b, 0:FULL * P, :].rearrange("(p t) d -> p t d", t=FULL)
                if b == 0:
                    sp.dma_start(buf[:, 0:4, 0:DC], full[:, 0:4, :]).then_inc(ctx_first, 16)
                    sp.dma_start(X[:], x_dram).then_inc(x_in, 16)
                    sp.dma_start(buf[:, 4:FULL, 0:DC], full[:, 4:FULL, :]).then_inc(ctx_in[0], 16)
                else:
                    sp.dma_start(buf[:, 0:FULL, 0:DC], full).then_inc(ctx_in[b % 2], 16)
                sp.dma_start(buf[0:TAIL, FULL, 0:DC], a["ctx_768"][b, FULL * P:S, :]).then_inc(ctx_in[b % 2], 16)
                if b == 0:
                    sp.dma_start(wq[:], a["t_Wq"].rearrange("(c p) n -> p c n", p=P)).then_inc(lat_in, 16)
                    sp.dma_start(wlkv[:], a["t_Wlkv"].rearrange("(c p) n -> p c n", p=P)).then_inc(lat_in, 16)
                    sp.dma_start(mask_in, a["p_mask"]).then_inc(mask_in_sem, 16)
                if b == 1:
                    sp.wait_ge(mask_ready, 1)
                    for k in range(B):
                        sp.dma_start(mask_row[32 * (k % 4):32 * (k % 4) + 1, k // 4, :].rearrange("o (p m) -> o p m", m=MPIECE),
                                     mask_flat[k * P // B:(k + 1) * P // B, :]).then_inc(mask_rows, 16)
                    for dst, src in (
                        (wo[:], a["t_Wo"].rearrange("(c p) n -> p c n", p=P)),
                        (bo[:], a["L0_xattn_bo"].rearrange("(o d) -> o d", o=1)),
                        (sums[:], a["c_sums"]), (pick[:], a["c_pick"]), (headsel[:], a["c_head"]),
                        (wx0[:], a["t_W_x0"].rearrange("(c p) n -> p c n", p=P)),
                        (wx2a[:], a["t_W_x2"][0:P, :]), (wx2b[:], a["t_W_x2"][P:160, :]),
                        (wr[:], a["t_W_r"].rearrange("(c p) n -> p c n", p=P)),
                        (wk[:], a["t_W_k"].rearrange("(c p) n -> p c n", p=P)),
                        (ww1[:], a["t_W_w1"].rearrange("(c p) n -> p c n", p=P)),
                        (ww2[0:64, :], a["t_W_w2"]), (ww2[64:65, :], a["L0_attn_b_w2"].rearrange("(o d) -> o d", o=1)),
                        (wv[:], a["t_W_v"].rearrange("(c p) n -> p c n", p=P)),
                        (wg[:], a["t_W_g"].rearrange("(c p) n -> p c n", p=P)),
                        (wo2[:], a["t_W_o"].rearrange("(c p) n -> p c n", p=P)),
                        (gnw[:], a["L0_attn_gn_weight"].rearrange("(o d) -> o d", o=1).broadcast_to([P, D])),
                        (gnb[:], a["L0_attn_gn_bias"].rearrange("(o d) -> o d", o=1).broadcast_to([P, D])),
                        (gatew[:], a["t_gate_w"].rearrange("(c p) n -> p c n", p=P)),
                        (ebias[:], a["L0_ffn_e_bias"].rearrange("(o d) -> o d", o=1).broadcast_to([P, NE])),
                        (before[:], a["c_before"].broadcast_to([P, NE * NE])),
                        (gbefore[:], a["c_gbefore"].broadcast_to([P, 16])),
                    ):
                        sp.dma_start(dst, src).then_inc(mixer_in, 16)
            sp.wait_ge(o_evac, 2 * NPAIR * B)
            sp.wait_ge(pT_evac, B * STEPS)
            for dst, src in (
                (eg[:, 0:NE], a["t_gate_proj"].rearrange("e (c p) i -> p e c i", p=P)),
                (eu[:, 0:NE], a["t_up_proj"].rearrange("e (c p) i -> p e c i", p=P)),
                (ed[:, 0:NE], a["t_down_proj"].rearrange("e i h -> i e h")),
                (eg[:, NE], a["t_shared_gate"].rearrange("(c p) i -> p c i", p=P)),
                (eu[:, NE], a["t_shared_up"].rearrange("(c p) i -> p c i", p=P)),
                (ed[:, NE], a["t_shared_down"]),
            ):
                    sp.dma_start(dst, src).then_inc(expert_in, 16)
            sp.wait_ge(acc_done, (NE + 1) * NT)
            sp.dma_start(out_dram, acc[:]).then_inc(stored, 16)
            sp.wait_ge(stored, 16)

        SETUP = 4 * 16
        LATENT = 2 * 16
        MIXER = 22 * 16
        EXPERT = 6 * 16

        @block.gpsimd
        def _(pool):
            tick = [0]

            def then(ins):
                tick[0] += 1
                ins.then_inc(pool_tick, 1)
                pool.wait_ge(pool_tick, tick[0])

            then(pool.memset(neg_half[:], -0.5))
            then(pool.memset(ones_row[:], 1.0))
            then(pool.memset(wt[64:65, :], 1.0))
            for i in range(NXH):
                then(pool.memset(xh[i][:, :, DC:DC + 1], 1.0))
            pool.memset(qb[:], 0.0).then_inc(pool_const, 1)
            pool.wait_ge(pool_const, 1)

            def rstd(n):
                lo, hi = NORMS[n]
                pool.wait_ge(ln_aggr, n + 1)
                then(pool.tensor_scalar(rs[:, lo:hi], mv[:, lo:hi, 1], LN_EPS, None, ALU.add))
                pool.tensor_tensor(rs[:, lo:hi], rs[:, lo:hi], neg_half[:, 0:hi - lo], ALU.pow).then_inc(ln_rstd, 1)

            def group_rstd(n):
                pool.wait_ge(caggr, n + 1)
                k, r = len(tiles(n % NG)), rows(tiles(n % NG)[0])
                then(pool.tensor_scalar(crs[0:r, n % 2, 0:k], cmv[0:r, n % 2, 0:k, 1], LN_EPS, None, ALU.add))
                pool.tensor_tensor(crs[0:r, n % 2, 0:k], crs[0:r, n % 2, 0:k], neg_half[0:r, 0:k], ALU.pow).then_inc(crstd, 1)

            group_rstd(0)
            group_rstd(1)

            def spread_mask(b):
                pool.wait_ge(k_r, b * NG + (2 if b else 6))
                if b == 0:
                    pool.wait_ge(mask_rows, 16 * B)
                if b >= 2:
                    pool.wait_ge(chunk_max, STEPS * (b - 1))
                pool.partition_broadcast(mask_bc[b % 2][:], mask_row[32 * (b % 4):32 * (b % 4) + 1, b // 4, :]).then_inc(mask_spread, 1)
                pool.wait_ge(mask_spread, b + 1)

            def mask_bias():
                pool.wait_ge(mask_in_sem, 16)
                pool.tensor_scalar(mask_flat[:], mask_in, 1.0, -MASKED, ALU.subtract, ALU.mult).then_inc(mask_ready, 1)
                pool.wait_ge(mask_ready, 1)

            def latent_rms(half):
                pool.wait_ge(lat_ss, 4 * (half + 1))
                of_half = lambda v: v[:].rearrange("p (j x) -> p j x", j=2)[:, :, 2 * H * half:2 * H * (half + 1)]
                then(pool.tensor_scalar(of_half(qkr), of_half(qkss), 1.0 / DH, 1e-16, ALU.mult, ALU.max))
                pool.tensor_tensor(of_half(qkr), of_half(qkr), neg_half[:, 0:4 * H].rearrange("p (j x) -> p j x", j=2), ALU.pow).then_inc(lat_r, 1)

            for u in range(steps):
                n = group_of(u)
                if u % STEPS == (2 if u >= STEPS else 6) and u // STEPS < B:
                    spread_mask(u // STEPS)
                if n is None:
                    continue
                if n + 2 < groups:
                    group_rstd(n + 2)
                pool.wait_ge(k_ss, n + 1)
                k, r = 4 * len(tiles(n % NG)), rows(tiles(n % NG)[0])
                then(pool.tensor_scalar(kr[0:r, n % 2, 0:k], kss[0:r, n % 2, 0:k], 1.0 / DH, 1e-16, ALU.mult, ALU.max))
                pool.tensor_tensor(kr[0:r, n % 2, 0:k], kr[0:r, n % 2, 0:k], neg_half[0:r, 0:k], ALU.pow).then_inc(k_r, 1)
                if u == 0:
                    rstd(0)
                if u == 1:
                    rstd(1)
                if u == 2:
                    mask_bias()
                if u in (4, 5):
                    latent_rms(u - 4)
            rstd(2)
            rstd(3)
            pool.wait_ge(r_mm, 1)
            pool.wait_ge(w1_mm, 1)
            pool.memset(aT, 0.0).then_inc(a_zero, 1)
            pool.wait_ge(a_zero, 1)
            for h in range(2):
                pool.wait_ge(g_act, h + 1)
                tl = slice(2 * h, 2 * h + 2)
                then(pool.tensor_tensor(sgb[:, tl, :], sg[:, tl, :], gnb[:].unsqueeze(1).broadcast_to([P, 2, D]), ALU.mult))
                pool.tensor_tensor(sg[:, tl, :], sg[:, tl, :], gnw[:].unsqueeze(1).broadcast_to([P, 2, D]), ALU.mult).then_inc(gain_ready, 1)
                pool.wait_ge(gain_ready, h + 1)
            for h in range(2):
                pool.wait_ge(gn_var, h + 1)
                part = slice(2 * H * h, 2 * H * (h + 1))
                then(pool.tensor_scalar(hs[:, 2, part], hs[:, 1, part], 1.0 / DH, LN_EPS, ALU.mult, ALU.add))
                pool.tensor_tensor(hs[:, 2, part], hs[:, 2, part], neg_half[:, 0:2 * H], ALU.pow).then_inc(gn_r, 1)
            rstd(4)
            rstd(5)

        @block.tensor
        def _(pe):
            def mm(out_, l, r, start=True, stop=True):
                return nc.tensor.matmul(out_, l, r, start=start, stop=stop)

            pe.wait_ge(setup_in, SETUP)
            for c in range(2):
                last = mm(ps[6][0:1, :], lnx_b[:, c:c + 1], wkv_raw[:, c, :], c == 0, c == 1)
            last.then_inc(wkv_bias, 1)

            LATENT_BANK = (2, 3, 6, 7)

            def turn_latents():
                pe.wait_ge(ln_out, 2 * NT)
                for i in range(NT):
                    for c in range(2):
                        last = nc.tensor.transpose(ps[c][:, i * P:(i + 1) * P], big[:, i, c * P:(c + 1) * P], ident[:])
                last.then_inc(tok_T, 1)

            def latent_queries(i):
                pe.wait_ge(tok_T_evac, 2)
                pe.wait_ge(lat_in, LATENT)
                bank = ps[LATENT_BANK[i]]
                for c in range(2):
                    mm(bank[:, 0:D], xT[:, c, i * P:(i + 1) * P], wq[:, c, :], c == 0, c == 1)
                for c in range(2):
                    last = mm(bank[:, D:2 * D], xT[:, c, i * P:(i + 1) * P], wlkv[:, c, 0:D], c == 0, c == 1)
                last.then_inc(lat_mm, 1)

            def latent_values(k):
                if k >= 2:
                    pe.wait_ge(vlat_evac, k - 1)
                for b in (2 * k, 2 * k + 1):
                    for c in range(2):
                        last = mm(ps[k % 2][0:T, (b % 2) * D:(b % 2 + 1) * D], xT[:, c, b * T:(b + 1) * T], wlkv[:, c, D:2 * D], c == 0, c == 1)
                last.then_inc(vlat_mm, 1)

            def turn_queries():
                pe.wait_ge(lat_n, 1)
                for j in range(2):
                    for pair in range(NPAIR):
                        for i in range(NT):
                            last = nc.tensor.transpose(ps[LATENT_BANK[2 * j + pair]][:, i * P:(i + 1) * P], qk[:, j, i, pair * P:(pair + 1) * P], ident[:])
                last.then_inc(lat_nT, 1)

            pe.wait_ge(wk_split, 3)

            turned, keys_turned = [0], [0]

            def turn_context(n):
                b, g = divmod(n, NG)
                pe.wait_ge(xh_ready, n + 1)
                if n:
                    pe.wait_ge(xhT_low, n)
                if keys_turned[0]:
                    pe.wait_ge(kT_evac, keys_turned[0])
                turned[0] = n + 1
                for i, t in enumerate(tiles(g)):
                    for c in range(2):
                        last = nc.tensor.transpose(tx_bank[0:W, c * 256 + i * P:c * 256 + i * P + rows(t)],
                                                   xh[b % NXH][0:rows(t), t, c * HALF:c * HALF + W], ident[0:rows(t), 0:rows(t)])
                last.then_inc(xhT_mm, 1)

            def keys(n):
                g = n % NG
                pe.wait_ge(xhT_low, n + 1)
                if n >= 1:
                    pe.wait_ge(k_evac, n)
                for i, t in enumerate(tiles(g)):
                    for s, (x_, w_) in enumerate(((xhT, wkh), (xhTl, wkh), (xhT, wkl))):
                        for c in range(2):
                            k = HALF + c
                            last = mm(k_bank[0:rows(t), i * D:(i + 1) * D], x_[n % 2][0:k, c, i * P:i * P + rows(t)], w_[0:k, c, :],
                                      s == 0 and c == 0, s == 2 and c == 1)
                last.then_inc(k_mm, 1)

            def turn_keys(n):
                g = n % NG
                pe.wait_ge(k_n, n + 1)
                pe.wait_ge(xhT_low, turned[0])
                if n:
                    pe.wait_ge(kT_evac, n)
                for i, t in enumerate(tiles(g)):
                    for pair in range(NPAIR):
                        last = nc.tensor.transpose(tx_bank[:, pair * 256 + i * P:pair * 256 + i * P + rows(t)],
                                                   kn[n % 2][0:rows(t), i * D + pair * P:i * D + (pair + 1) * P], ident[0:rows(t), 0:rows(t)])
                last.then_inc(kT_mm, 1)
                keys_turned[0] = n + 1

            def scores(m):
                b, k = divmod(m, STEPS)
                pair, c = divmod(k, NCH)
                lo, hi = span(c)
                if m >= NCH:
                    pe.wait_ge(chunk_max, m - NCH + 1)
                pe.wait_ge(kT_evac, b * NG + min(2 * c + 2, NG))
                bank = score_bank[c][:, 0:hi - lo]
                q = qb[:, b * NPAIR + pair, :]
                if hi <= S:
                    last = mm(bank, q, kT[b % 2][:, pair, lo:hi])
                else:
                    mm(bank[:, 0:S - lo], q, kT[b % 2][:, pair, lo:S])
                    last = mm(bank[:, S - lo:hi - lo], q, klT[:, pair, b * T:(b + 1) * T])
                last.then_inc(score_mm, 1)

            def turn_probs(m):
                c = m % NCH
                j = m // NCH
                pe.wait_ge(exp_done, m + 1)
                if m >= 1:
                    pe.wait_ge(pT_evac, m)
                for i, (t, lo, hi) in enumerate(key_tiles(c)):
                    last = nc.tensor.transpose(tp_bank[0:hi - lo, i * P:(i + 1) * P], pr[j % 2][:, lo:hi], ident[:])
                if c == NCH - 1:
                    pe.wait_ge(plat_ready, j + 1)
                    last = nc.tensor.transpose(tp_bank[0:T, P:2 * P], plat[:], ident[:])
                last.then_inc(pT_mm, 1)

            def context_sum(m):
                b = m // STEPS
                c = m % NCH
                j = m // NCH
                pe.wait_ge(pT_evac, m + 1)
                if c == 0 and j >= 1:
                    pe.wait_ge(y_evac, j)
                for i, (t, lo, hi) in enumerate(key_tiles(c)):
                    last = mm(y_bank[:, 0:DC + 1], pT[m % 2][0:hi - lo, i, :], xh[b % NXH][0:hi - lo, t, 0:DC + 1], t == 0, t == FULL)
                if c == NCH - 1:
                    last.then_inc(y_mm, 1)

            def turn_sum(j):
                pe.wait_ge(y_evac, j + 1)
                pe.wait_ge(pT_evac, NCH * (j + 1) + (1 if NCH * (j + 1) < chunks else 0))
                nc.tensor.transpose(tp_bank[0:HALF, 0:P], ysb[:, 0:HALF], ident[:])
                nc.tensor.transpose(tp_bank[0:W, P:2 * P], ysb[:, HALF:DC + 1], ident[:]).then_inc(yT_mm, 1)

            def head_out(j):
                b, pair = divmod(j, NPAIR)
                pe.wait_ge(yT_evac, 2 * (j + 1))
                if NCH * (j + 1) + 1 < chunks:
                    pe.wait_ge(pT_evac, NCH * (j + 1) + 2)
                bank = tp_bank[:, 0:P]
                cols = slice(D + pair * P, D + (pair + 1) * P)
                mm(bank, wkv[0:HALF, 0, cols], yT[0:HALF, 0, :], True, False)
                mm(bank, wkv[0:W, 1, cols], yT[0:W, 1, :], False, False)
                mm(bank, vlat[:, b, pair * P:(pair + 1) * P], plT[:], False, True).then_inc(o_mm, 1)

            def project(half):
                pe.wait_ge(o_evac, NPAIR * B * (half + 1))
                if half == 0:
                    pe.wait_ge(mixer_in, MIXER)
                    pe.wait_ge(k_evac, groups)
                else:
                    pe.wait_ge(res_add, 1)
                for i in (2 * half, 2 * half + 1):
                    bank = k_bank[:, (i % 2) * D:(i % 2 + 1) * D]
                    for c in range(NPAIR):
                        mm(bank, oT[:, c, i * P:(i + 1) * P], wo[:, c, :], c == 0, False)
                    last = mm(bank, ones_row[:], bo[:], False, True)
                last.then_inc(res_mm, 1)

            def turn_tokens(k, bank):
                pe.wait_ge(ln_out, normed(2 + k))
                for i in (2 * (k % 2), 2 * (k % 2) + 1):
                    for c in range(2):
                        last = nc.tensor.transpose(bank[:, c * 2 * P + (i % 2) * P:c * 2 * P + (i % 2 + 1) * P], big[:, i, c * P:(c + 1) * P], ident[:])
                last.then_inc(tok_T, 1)

            def first_rates(half):
                part = slice(half * 2 * P, (half + 1) * 2 * P)
                pe.wait_ge(xx_ready, 2 * (half + 1))
                for c in range(2):
                    mm(ps[2 * half][:, 0:2 * P], wx0[:, c, 0:P], mixed[0][:, c, part], c == 0, c == 1)
                for c in range(2):
                    last = mm(ps[2 * half + 1][0:32, 0:2 * P], wx0[:, c, P:160], mixed[0][:, c, part], c == 0, c == 1)
                last.then_inc(xp_mm, 1)

            turn_context(0)
            for u in range(steps):
                n, m = group_of(u), chunk_of(u)
                prev = group_of(u - 2) if u >= 2 else None
                if prev is not None:
                    turn_keys(prev)
                if n is not None:
                    keys(n)
                m6, m7 = lag(u, 6), lag(u, 7)
                if m6 is not None and m6 % NCH == NCH - 1:
                    turn_sum(m6 // NCH)
                if m7 is not None and m7 % NCH == NCH - 1:
                    head_out(m7 // NCH)
                if n is not None and n + 1 < groups:
                    turn_context(n + 1)
                if m == 0:
                    pe.wait_ge(lat_nT_evac, 1)
                    pe.wait_ge(vlat_evac, 4)
                if m is not None:
                    scores(m)
                if m6 is not None and m6 % NCH == NCH - 1:
                    pe.wait_ge(yT_evac, 2 * (m6 // NCH + 1))
                if m7 is not None and m7 % NCH == NCH - 1:
                    pe.wait_ge(o_evac, 2 * (m7 // NCH + 1))
                if lag(u, 4) is not None:
                    turn_probs(lag(u, 4))
                if lag(u, 5) is not None:
                    context_sum(lag(u, 5))
                if u == 3:
                    turn_latents()
                if u in (4, 5):
                    latent_queries(2 * (u - 4))
                    latent_queries(2 * (u - 4) + 1)
                if u in (6, 7):
                    latent_values(2 * (u - 6))
                    latent_values(2 * (u - 6) + 1)
                if u == 7:
                    turn_queries()
                if u == B * STEPS + 2:
                    project(0)
                if u == B * STEPS + 4:
                    turn_tokens(0, tx_bank)

            first_rates(0)
            project(1)
            turn_tokens(1, tx_bank)
            first_rates(1)
            pe.wait_ge(xp_act, 4)
            def rates(k):
                i = ORDER[k]
                for c in range(2):
                    s = 2 * k + c
                    if s >= 4:
                        pe.wait_ge(mu_use, s - 3)
                    if i < 4:
                        l, r = wx2a[32 * i:32 * i + 32, c * P:(c + 1) * P], xpa[32 * i:32 * i + 32, :]
                    else:
                        l, r = wx2b[:, c * P:(c + 1) * P], xpb[:]
                    nc.tensor.matmul(ps[s % 4][:], l, r, start=True, stop=True, tile_position=(32 * (i % 4), 0)).then_inc(mu_mm, 1)

            rates(0)
            rates(1)
            pe.wait_ge(mixed_ready, 2)
            for c in range(2):
                last = mm(ps[5][0:64, :], ww1[:, c, :], mixed[1][:, c, :], c == 0, c == 1)
            last.then_inc(w1_mm, 1)
            rates(2)
            pe.wait_ge(mixed_ready, 4)
            for c in range(2):
                last = mm(ps[4][:], wr[:, c, :], mixed[0][:, c, :], c == 0, c == 1)
            last.then_inc(r_mm, 1)
            rates(3)
            pe.wait_ge(w1_act, 1)
            for i in range(NT):
                last = mm(ps[7][:, i * P:(i + 1) * P], wt[:, i * P:(i + 1) * P], ww2[:])
            last.then_inc(w2_mm, 1)
            pe.wait_ge(mixed_ready, 6)
            for c in range(2):
                last = mm(ps[6][:], wk[:, c, :], mixed[2][:, c, :], c == 0, c == 1)
            last.then_inc(kk_mm, 1)
            rates(4)
            pe.wait_ge(w2_act, 1)
            pe.wait_ge(r_evac, 1)
            pe.wait_ge(kk_evac, 1)
            for half in range(2):
                for i in range(NT):
                    s = NT * half + i
                    if s >= 4:
                        pe.wait_ge(e_act, s - 3)
                    mm(ps[4 + s % 4][:, 0:3 * P], ew[:, i, :], sums[:, 3 * half:3 * half + 3, :].rearrange("p l n -> p (l n)")).then_inc(e_mm, 1)
            pe.wait_ge(mu_use, 10)
            pe.wait_ge(mixed_ready, 8)
            for i in range(NT):
                for c in range(2):
                    last = mm(ps[i // 2][:, (i % 2) * D:(i % 2 + 1) * D], mixed[3][:, c, i * P:(i + 1) * P], wv[:, c, :], c == 0, c == 1)
                if i % 2:
                    last.then_inc(v_mm, 1)
            pe.wait_ge(mixed_ready, 10)
            for i in range(NT):
                for c in range(2):
                    last = mm(ps[2 + i // 2][:, (i % 2) * D:(i % 2 + 1) * D], mixed[4][:, c, i * P:(i + 1) * P], wg[:, c, :], c == 0, c == 1)
                if i % 2:
                    last.then_inc(g_mm, 1)
            pe.wait_ge(ruk_ready, 1)
            pe.wait_ge(e_act, 2 * NT)
            for i in range(NT):
                last = mm(ps[7][:, 4 * i:4 * i + 4], ruk[:, i * P:(i + 1) * P], headsel[:])
            last.then_inc(dc_mm, 1)
            pe.wait_ge(v_evac, 2)
            pe.wait_ge(g_act, 2)

            def weights(k):
                i, half = divmod(k, 2)
                first = 4 * (k % 2)
                if k >= 2:
                    pe.wait_ge(a_pick, LEVELS // 2 * (k - 1))
                if k == 1:
                    pe.wait_ge(vec, 1)
                if k == 5:
                    pe.wait_ge(av_read, 1)
                for j in range(LEVELS // 2):
                    lv = LEVELS // 2 * half + j
                    if i == 0:
                        pe.wait_ge(level_ready, 2 * (lv + 1))
                    for h in range(H):
                        op = ex[32 * h:32 * h + 32, lv, i * P:(i + 1) * P]
                        last = nc.tensor.matmul(ps[first + h][:, j * P:(j + 1) * P], op, op, start=True, stop=True, tile_position=(32 * h, 0))
                last.then_inc(a_mm, 1)

            def weigh(half):
                pe.wait_ge(a_zero, 1)
                pe.wait_ge(a_pick, 2 * LEVELS * (half + 1))
                for i in (2 * half, 2 * half + 1):
                    for h in range(H):
                        last = mm(ps[4 + half][:, (i % 2) * D + h * DH:(i % 2) * D + (h + 1) * DH], aT[:, i, h, :], vn[:, i, h * DH:(h + 1) * DH])
                last.then_inc(av_mm, 1)

            def turn_gated(half):
                pe.wait_ge(o_gated, half + 1)
                for i in (2 * half, 2 * half + 1):
                    for c in range(2):
                        last = nc.tensor.transpose(ps[6 + half][:, c * 2 * P + (i % 2) * P:c * 2 * P + (i % 2 + 1) * P], on[:, i, c * P:(c + 1) * P], ident[:])
                last.then_inc(oT2_mm, 1)

            def project_mixer(half):
                pe.wait_ge(oT2_evac, half + 1)
                for i in (2 * half, 2 * half + 1):
                    for c in range(2):
                        last = mm(ps[2 + half][:, (i % 2) * D:(i % 2 + 1) * D], oT2[:, c, i * P:(i + 1) * P], wo2[:, c, :], c == 0, c == 1)
                last.then_inc(res_mm, 1)

            for k in range(5):
                weights(k)
            weigh(0)
            for k in range(5, 8):
                weights(k)
            weigh(1)
            for half in range(2):
                turn_gated(half)
                project_mixer(half)
            turn_tokens(2, ps[0])
            turn_tokens(3, ps[1])
            pe.wait_ge(tok_T_evac, 6)
            for i in range(NT):
                for c in range(2):
                    last = mm(ps[6][:, i * NE:(i + 1) * NE], xT[:, c, i * P:(i + 1) * P], gatew[:, c, :], c == 0, c == 1)
            last.then_inc(gate_mm, 1)
            pe.wait_ge(expert_in, EXPERT)
            pe.wait_ge(res_add, 4)

            def down(e):
                pe.wait_ge(inter_ready, e + 1)
                for i in range(NT):
                    if e >= 2 and i % 2 == 0:
                        pe.wait_ge(acc_done, (e - 2) * NT + i + 2)
                    last = mm(ps[4 + 2 * (e % 2) + i // 2][:, (i % 2) * D:(i % 2 + 1) * D], inter[e % 2][:, i * P:(i + 1) * P], ed[:, e, :])
                    if i % 2:
                        last.then_inc(down_mm, 1)

            for e in range(NE + 1):
                if e >= 2:
                    pe.wait_ge(inter_ready, e - 1)
                for j, w_ in enumerate((eg, eu)):
                    for c in range(2):
                        last = mm(ps[2 * (e % 2) + j][:], w_[:, e, c, :], xT[:, c, :], c == 0, c == 1)
                    last.then_inc(gu_mm, 1)
                if e >= 1:
                    down(e - 1)
            down(NE)

        @block.scalar
        def _(act):
            A = nc.scalar.activation
            def evac_latents():
                act.wait_ge(setup_in, SETUP)
                act.wait_ge(tok_T, 1)
                for c in range(2):
                    A(xT[:, c, :], ps[c][:], ACT.Identity, bias=lnl_b[:, c:c + 1], scale=lnl_g[:, c:c + 1]).then_inc(tok_T_evac, 1)

            def square_latents(i):
                act.wait_ge(lat_mm, i + 1)
                A(kn_sq(i), ps[(2, 3, 6, 7)[i]][:], ACT.Square).then_inc(lat_sq, 1)

            def evac_values(k):
                act.wait_ge(vlat_mm, k + 1)
                A(vlat[:, 2 * k:2 * k + 2, :], ps[k % 2][0:T, :], ACT.Copy).then_inc(vlat_evac, 1)

            def evac_queries():
                act.wait_ge(lat_nT, 1)
                for pair in range(NPAIR):
                    for h in range(2):
                        part = slice(h * DH, (h + 1) * DH)
                        A(qb[part, pair::NPAIR, h * T:(h + 1) * T], ps[2 + pair][part, :].rearrange("p (b t) -> p b t", b=B), ACT.Copy,
                          scale=qkg[part, 0:1])
                    last = A(klT[:, pair, :], ps[6 + pair][:], ACT.Copy)
                last.then_inc(lat_nT_evac, 1)

            def evac_context(n):
                act.wait_ge(xhT_mm, n + 1)
                k = 256 if n % NG < NG - 1 else TAIL
                A(xhT[n % 2][:, :, 0:k], tx_bank[0:W, :].rearrange("p (c k) -> p c k", c=2)[:, :, 0:k], ACT.Copy).then_inc(xhT_evac, 1)

            def square_keys(n):
                act.wait_ge(k_mm, n + 1)
                if n >= 1:
                    act.wait_ge(k_ss, n)
                r, k = rows(tiles(n % NG)[0]), D * len(tiles(n % NG))
                A(ksq[0:r, 0:k], k_bank[0:r, 0:k], ACT.Square).then_inc(k_sq, 1)

            def copy_keys(n):
                if n >= 2:
                    act.wait_ge(k_n, n - 1)
                r, k = rows(tiles(n % NG)[0]), D * len(tiles(n % NG))
                A(kraw[n % 2][0:r, 0:k], k_bank[0:r, 0:k], ACT.Copy).then_inc(k_evac, 1)

            def evac_keys(n):
                b, g = divmod(n, NG)
                act.wait_ge(kT_mm, n + 1)
                k = 256 if g < NG - 1 else TAIL
                A(kT[b % 2][:, :, 256 * g:256 * g + k], tx_bank[:].rearrange("p (c k) -> p c k", c=2)[:, :, 0:k], ACT.Copy).then_inc(kT_evac, 1)

            def exponentials(m):
                j, c = divmod(m, NCH)
                act.wait_ge(row_max, j + 1)
                lo, hi = span(c)
                A(pr[j % 2][:, lo:hi], pr[j % 2][:, lo:hi], ACT.Exp, bias=nm[:, j % 2:j % 2 + 1], accum_out=ls[:, j % 2, c:c + 1]).then_inc(exp_done, 1)

            def evac_probs(m):
                c = m % NCH
                act.wait_ge(pT_mm, m + 1)
                if c < NCH - 1:
                    A(pT[m % 2].rearrange("p i q -> p (i q)"), tp_bank[:], ACT.Copy).then_inc(pT_evac, 1)
                else:
                    A(plT[:], tp_bank[0:T, P:2 * P], ACT.Copy)
                    A(pT[m % 2][0:TAIL, 0, :], tp_bank[0:TAIL, 0:P], ACT.Copy).then_inc(pT_evac, 1)

            def evac_tokens(k, bank):
                act.wait_ge(tok_T, 2 + k)
                A(xT[:, :, (k % 2) * 2 * P:(k % 2 + 1) * 2 * P], bank[:].rearrange("p (c k) -> p c k", c=2), ACT.Copy).then_inc(tok_T_evac, 1)

            def first_tanh(half):
                part = slice(half * 2 * P, (half + 1) * 2 * P)
                act.wait_ge(xp_mm, half + 1)
                A(xpa[:, part], ps[2 * half][:, 0:2 * P], ACT.Tanh).then_inc(xp_act, 1)
                A(xpb[:, part], ps[2 * half + 1][0:32, 0:2 * P], ACT.Tanh).then_inc(xp_act, 1)

            evac_context(0)
            for u in range(steps):
                n = group_of(u)
                prev = group_of(u - 2) if u >= 2 else None
                if prev is not None:
                    evac_keys(prev)
                m4 = lag(u, 4)
                if m4 is not None and m4 % NCH < NCH - 1:
                    exponentials(m4)
                    if m4 % NCH == NCH - 2:
                        exponentials(m4 + 1)
                m6, m7 = lag(u, 6), lag(u, 7)
                if m6 is not None and m6 % NCH == NCH - 1:
                    j = m6 // NCH
                    act.wait_ge(yT_mm, j + 1)
                    A(yT[0:HALF, 0, :], tp_bank[0:HALF, 0:P], ACT.Copy).then_inc(yT_evac, 1)
                    A(yT[:, 1, :], tp_bank[0:W, P:2 * P], ACT.Copy).then_inc(yT_evac, 1)
                if m7 is not None and m7 % NCH == NCH - 1:
                    j = m7 // NCH
                    b, pair = divmod(j, NPAIR)
                    act.wait_ge(o_mm, j + 1)
                    for h in range(2):
                        part = slice(h * DH, (h + 1) * DH)
                        A(oT[part, pair, b * T:(b + 1) * T], tp_bank[part, h * T:(h + 1) * T], ACT.Copy).then_inc(o_evac, 1)
                if n is not None:
                    square_keys(n)
                    if n + 1 < groups:
                        evac_context(n + 1)
                    copy_keys(n)
                if m4 is not None:
                    evac_probs(m4)
                if u == 3:
                    evac_latents()
                if u in (4, 5):
                    square_latents(2 * (u - 4))
                    square_latents(2 * (u - 4) + 1)
                if u in (6, 7):
                    evac_values(2 * (u - 6))
                    evac_values(2 * (u - 6) + 1)
                if u == 7:
                    evac_queries()
                if u == B * STEPS + 4:
                    evac_tokens(0, tx_bank)

            act.wait_ge(mixer_in, MIXER)
            first_tanh(0)
            evac_tokens(1, tx_bank)
            first_tanh(1)
            act.wait_ge(w1_mm, 1)
            A(wt[0:64, :], ps[5][0:64, :], ACT.Tanh).then_inc(w1_act, 1)
            act.wait_ge(r_mm, 1)
            A(rT[:], ps[4][:], ACT.Copy).then_inc(r_evac, 1)
            act.wait_ge(w2_mm, 1)
            A(ew[:], ps[7][:], ACT.Exp).then_inc(w2_act, 1)
            act.wait_ge(kk_mm, 1)
            A(rkT[:], ps[6][:], ACT.Copy).then_inc(kk_evac, 1)
            for s in range(2 * NT):
                half, i = divmod(s, NT)
                act.wait_ge(e_mm, s + 1)
                A(ex[:, 3 * half:3 * half + 3, i * P:(i + 1) * P], ps[4 + s % 4][:, 0:3 * P].rearrange("p (l n) -> p l n", l=3), ACT.Exp, scale=-1.0).then_inc(e_act, 1)
            for j in range(2):
                act.wait_ge(v_mm, j + 1)
                A(vn[:, 2 * j:2 * j + 2, :], ps[j][:], ACT.Copy).then_inc(v_evac, 1)
            for j in range(2):
                act.wait_ge(g_mm, j + 1)
                A(sg[:, 2 * j:2 * j + 2, :], ps[2 + j][:], ACT.Silu).then_inc(g_act, 1)
            for half in range(2):
                tl = slice(2 * half, 2 * half + 2)
                act.wait_ge(o_cent, half + 1)
                A(big[:, tl, :], on[:, tl, :], ACT.Square).then_inc(o_sq, 1)
            for half in range(2):
                act.wait_ge(oT2_mm, half + 1)
                A(oT2[:, :, half * 2 * P:(half + 1) * 2 * P], ps[6 + half][:].rearrange("p (c k) -> p c k", c=2), ACT.Copy).then_inc(oT2_evac, 1)
            evac_tokens(2, ps[0])
            evac_tokens(3, ps[1])
            act.wait_ge(gate_mm, 1)
            A(fe[:, 0], ps[6][:, 0:NT * NE], ACT.Exp, scale=-1.0).then_inc(gate_exp, 1)
            for e in range(NE + 1):
                act.wait_ge(gu_mm, 2 * e + 1)
                if e >= 2:
                    act.wait_ge(inter_ready, e - 1)
                A(sil[e % 2][:], ps[2 * (e % 2)][:], ACT.Silu).then_inc(silu, 1)

        @block.vector
        def _(dve):
            V = nc.vector
            tick = [0]

            def then(ins):
                tick[0] += 1
                ins.then_inc(vec_tick, 1)
                dve.wait_ge(vec_tick, tick[0])

            def norm_stats(n, src):
                lo, hi = NORMS[n]
                for i in range(lo, hi):
                    V.bn_stats(st[:, i, :], src[:, i, :]).then_inc(ln_stats, 1)
                dve.wait_ge(ln_stats, normed(n))
                for i in range(lo, hi):
                    last = V.bn_aggr(mv[:, i, :], st[:, i, :])
                last.then_inc(ln_aggr, 1)

            def norm_apply(n, src, dst):
                dve.wait_ge(ln_rstd, n + 1)
                for i in range(*NORMS[n]):
                    V.tensor_scalar(dst[:, i, :], src[:, i, :], mv[:, i, 0:1], rs[:, i:i + 1], ALU.subtract, ALU.mult).then_inc(ln_out, 1)

            def norm_tokens(n, src, dst):
                norm_stats(n, src)
                norm_apply(n, src, dst)

            dve.wait_ge(setup_in, SETUP)
            for c in range(2):
                V.tensor_scalar(wkv[0:HALF, c, :], wkv_raw[:, c, :], lnx_g[:, c:c + 1], None, ALU.mult)
            V.scalar_tensor_tensor(qkg[:], qg[:], DH ** -0.5, kg[:], ALU.mult, ALU.mult)
            dve.wait_ge(wkv_bias, 1)
            V.tensor_copy(wkv[HALF:W, 1, :], ps[6][0:1, :]).then_inc(wkv_ready, 1)
            dve.wait_ge(wkv_ready, 1)
            parts = ((slice(0, HALF), 0), (slice(0, W), 1))
            for p_, c in parts:
                V.tensor_copy(wkh[p_, c, :], wkv[p_, c, 0:D]).then_inc(wk_split, 1)
            dve.wait_ge(wk_split, 2)
            for p_, c in parts:
                last = V.tensor_tensor(wkl[p_, c, :], wkv[p_, c, 0:D], wkh[p_, c, :].bitcast(F32), ALU.subtract)
            last.then_inc(wk_split, 1)

            def group_stats(n):
                b, g = divmod(n, NG)
                if n == 0:
                    dve.wait_ge(ctx_first, 16)
                if g == (0 if b else 2):
                    dve.wait_ge(ctx_in[b % 2], 32 * (b // 2 + 1))
                for i, t in enumerate(tiles(g)):
                    last = V.bn_stats(cst[0:rows(t), n % 2, i, :], xh[b % NXH][0:rows(t), t, 0:DC])
                last.then_inc(cstat, 1)
                dve.wait_ge(cstat, n + 1)
                for i, t in enumerate(tiles(g)):
                    last = V.bn_aggr(cmv[0:rows(t), n % 2, i, :], cst[0:rows(t), n % 2, i, :])
                last.then_inc(caggr, 1)

            def normalise(n):
                b, g = divmod(n, NG)
                dve.wait_ge(crstd, n + 1)
                for i, t in enumerate(tiles(g)):
                    r = rows(t)
                    last = V.tensor_scalar(xh[b % NXH][0:r, t, 0:DC], xh[b % NXH][0:r, t, 0:DC], cmv[0:r, n % 2, i, 0:1], crs[0:r, n % 2, i:i + 1], ALU.subtract, ALU.mult)
                last.then_inc(xh_ready, 1)

            dve.wait_ge(pool_const, 1)
            group_stats(0)
            group_stats(1)
            normalise(0)
            normalise(1)

            def latent_sums(i):
                dve.wait_ge(lat_sq, i + 1)
                sq = kn_sq(i).rearrange("p (j h d) -> p j h d", j=2, h=H)
                for j in range(2):
                    V.tensor_reduce(qkss[:, (j * NT + i) * H:(j * NT + i + 1) * H], sq[:, j], AX.X, ALU.add).then_inc(lat_ss, 1)

            def scale_latents():
                dve.wait_ge(lat_r, 2)
                for i in range(NT):
                    for j in range(2):
                        last = V.tensor_tensor(qk[:, j, i, :].rearrange("p (h d) -> p h d", h=H),
                                               ps[(2, 3, 6, 7)[i]][:, j * D:(j + 1) * D].rearrange("p (h d) -> p h d", h=H),
                                               qkr[:, (j * NT + i) * H:(j * NT + i + 1) * H].unsqueeze(2).broadcast_to([P, H, DH]), ALU.mult)
                last.then_inc(lat_n, 1)

            def key_sums(n):
                dve.wait_ge(k_sq, n + 1)
                r, k = rows(tiles(n % NG)[0]), len(tiles(n % NG))
                V.tensor_reduce(kss[0:r, n % 2, 0:4 * k], ksq[0:r, 0:D * k].rearrange("p (h d) -> p h d", d=DH), AX.X, ALU.add).then_inc(k_ss, 1)

            def scale_keys(n):
                dve.wait_ge(k_r, n + 1)
                dve.wait_ge(k_evac, n + 1)
                if n >= 2:
                    dve.wait_ge(kT_mm, n - 1)
                r, k = rows(tiles(n % NG)[0]), len(tiles(n % NG))
                V.tensor_tensor(kn[n % 2][0:r, 0:D * k].rearrange("p (h d) -> p h d", d=DH), kraw[n % 2][0:r, 0:D * k].rearrange("p (h d) -> p h d", d=DH),
                                kr[0:r, n % 2, 0:4 * k].unsqueeze(2).broadcast_to([r, 4 * k, DH]), ALU.mult).then_inc(k_n, 1)

            def split_context(n):
                dve.wait_ge(xhT_evac, n + 1)
                k = 256 if n % NG < NG - 1 else TAIL
                turned = tx_bank[0:W, :].rearrange("p (c k) -> p c k", c=2)[:, :, 0:k]
                V.tensor_tensor(xhTl[n % 2][:, :, 0:k], turned, xhT[n % 2][:, :, 0:k].bitcast(F32), ALU.subtract).then_inc(xhT_low, 1)

            def maxima(m):
                j, c = divmod(m, NCH)
                lo, hi = span(c)
                dve.wait_ge(score_mm, m + 1)
                if j % NPAIR == 0 and c == 0:
                    dve.wait_ge(mask_spread, j // NPAIR + 1)
                V.tensor_tensor_reduce(pr[j % 2][:, lo:hi], score_bank[c][:, 0:hi - lo], mask_bc[(j // NPAIR) % 2][:, lo:hi], 1.0, LOWEST,
                                       ALU.add, ALU.max, mx[:, j % 2, c:c + 1]).then_inc(chunk_max, 1)
                if c == NCH - 1:
                    dve.wait_ge(chunk_max, m + 1)
                    V.tensor_reduce(nm[:, j % 2:j % 2 + 1], mx[:, j % 2, :], AX.X, ALU.max, negate=True).then_inc(row_max, 1)

            def latent_probs(j):
                dve.wait_ge(exp_done, NCH * (j + 1))
                V.tensor_reduce(lsum[:, j % 2:j % 2 + 1], ls[:, j % 2, :], AX.X, ALU.add).then_inc(row_sum, 1)
                dve.wait_ge(row_sum, j + 1)
                V.reciprocal(rl[:, j % 2:j % 2 + 1], lsum[:, j % 2:j % 2 + 1]).then_inc(row_inv, 1)
                dve.wait_ge(row_inv, j + 1)
                V.tensor_scalar(plat[:], pr[j % 2][:, S:KEYS], rl[:, j % 2:j % 2 + 1], None, ALU.mult).then_inc(plat_ready, 1)

            def evac_sum(j):
                dve.wait_ge(y_mm, j + 1)
                V.tensor_scalar(ysb[:, 0:DC + 1], y_bank[:, 0:DC + 1], rl[:, j % 2:j % 2 + 1], None, ALU.mult).then_inc(y_evac, 1)

            def residual(half):
                tl = slice(2 * half, 2 * half + 2)
                dve.wait_ge(res_mm, half + 1)
                V.tensor_tensor(X[:, tl, :], X[:, tl, :], k_bank[:].rearrange("p (i d) -> p i d", i=2), ALU.add).then_inc(res_add, 1)
                dve.wait_ge(res_add, half + 1)
                norm_tokens(2 + half, X, big)

            def differences(half):
                dve.wait_ge(tok_T_evac, 3 + half)
                part = slice(half * 2 * P, (half + 1) * 2 * P)
                for c in range(2):
                    xv = xT[:, c, part].rearrange("p (b t) -> p b t", t=T)
                    dv = delta[:, c, part].rearrange("p (b t) -> p b t", t=T)
                    V.tensor_tensor(dv[:, :, 1:T], xv[:, :, 0:T - 1], xv[:, :, 1:T], ALU.subtract)
                    V.tensor_scalar(dv[:, :, 0:1], xv[:, :, 0:1], -1.0, None, ALU.mult).then_inc(d_ready, 1)
                for c in range(2):
                    dve.wait_ge(d_ready, 2 * half + c + 1)
                    V.scalar_tensor_tensor(mixed[0][:, c, part], delta[:, c, part], mu0[:, c:c + 1], xT[:, c, part], ALU.mult, ALU.add).then_inc(xx_ready, 1)

            split_context(0)
            for u in range(steps):
                n, m = group_of(u), chunk_of(u)
                m4, m5 = lag(u, 4), lag(u, 5)
                prev = group_of(u - 1) if u else None
                if m4 is not None and m4 % NCH == NCH - 1:
                    latent_probs(m4 // NCH)
                if n is not None and n + 2 < groups:
                    group_stats(n + 2)
                if prev is not None:
                    scale_keys(prev)
                if n is not None:
                    key_sums(n)
                    if n + 1 < groups:
                        split_context(n + 1)
                    if n + 2 < groups:
                        normalise(n + 2)
                if m is not None:
                    maxima(m)
                if m5 is not None and m5 % NCH == NCH - 1:
                    evac_sum(m5 // NCH)
                if u == 0:
                    dve.wait_ge(x_in, 16)
                    norm_stats(0, X)
                if u == 1:
                    norm_apply(0, X, xn)
                    dve.wait_ge(ln_out, NT)
                    norm_stats(1, xn)
                if u == 2:
                    norm_apply(1, xn, big)
                if u in (4, 5):
                    latent_sums(2 * (u - 4))
                    latent_sums(2 * (u - 4) + 1)
                if u == 6:
                    scale_latents()
                if u == B * STEPS + 2:
                    residual(0)

            differences(0)
            residual(1)
            differences(1)
            for k, i in enumerate(ORDER):
                for c in range(2):
                    s = 2 * k + c
                    dve.wait_ge(mu_mm, s + 1)
                    V.scalar_tensor_tensor(tmix[s % 2][:], ps[s % 4][:], xbias[:, c, i:i + 1], delta[:, c, :], ALU.add, ALU.mult).then_inc(mu_use, 1)
                    dve.wait_ge(mu_use, s + 1)
                    V.tensor_tensor(mixed[i][:, c, :], tmix[s % 2][:], xT[:, c, :], ALU.add).then_inc(mixed_ready, 1)
            dve.wait_ge(r_evac, 1)
            dve.wait_ge(kk_evac, 1)
            V.scalar_tensor_tensor(ruk[:], rT[:], bonus[:, 0:1], rkT[:], ALU.mult, ALU.mult).then_inc(ruk_ready, 1)
            for lv in range(LEVELS):
                if lv % 3 == 0:
                    dve.wait_ge(e_act, NT * (lv // 3 + 1))
                ev = ex[:, lv, :].rearrange("p (n s m) -> p n s m", s=2, m=1 << lv)
                for side, src in ((1, rT), (0, rkT)):
                    sv = src[:].rearrange("p (n s m) -> p n s m", s=2, m=1 << lv)
                    V.tensor_tensor(ev[:, :, side], ev[:, :, side], sv[:, :, side], ALU.mult).then_inc(level_ready, 1)
            dve.wait_ge(dc_mm, 1)
            V.tensor_copy(dcoef[:], ps[7][:, 0:4 * NT]).then_inc(vec, 1)

            def heads(t_, half):
                return t_[:, 2 * half:2 * half + 2, :].rearrange("p i (h d) -> p (i h) d", h=H)

            def pick_weights(k):
                i, half = divmod(k, 2)
                dve.wait_ge(a_mm, k + 1)
                for j in range(LEVELS // 2):
                    lv = LEVELS // 2 * half + j
                    if i + lv:
                        dve.wait_ge(a_pick, i * LEVELS + lv)
                    for h in range(H):
                        halves = lambda v: v.rearrange("p (n s m) -> p n s m", s=2, m=1 << lv)[:, :, 1, :]
                        last = V.copy_predicated(halves(aT[:, i, h]), pick[:, lv, :].rearrange("p (n m) -> p n m", m=1 << lv),
                                                 halves(ps[4 * (k % 2) + h][:, j * P:(j + 1) * P]))
                    last.then_inc(a_pick, 1)

            def centre(half):
                part = slice(2 * H * half, 2 * H * (half + 1))
                own = dcoef[:, 2 * half:2 * half + 2, :].rearrange("p i h -> p (i h)").unsqueeze(2).broadcast_to([P, 2 * H, DH])
                then(V.tensor_tensor(heads(on, half), heads(vn, half), own, ALU.mult))
                dve.wait_ge(av_mm, half + 1)
                V.tensor_tensor(heads(on, half), heads(on, half), ps[4 + half][:].rearrange("p (h d) -> p h d", d=DH), ALU.add).then_inc(av_read, 1)
                dve.wait_ge(av_read, half + 1)
                then(V.tensor_reduce(hs[:, 0, part], heads(on, half), AX.X, ALU.add))
                then(V.tensor_scalar(hs[:, 3, part], hs[:, 0, part], 1.0 / DH, None, ALU.mult))
                V.tensor_tensor(heads(on, half), heads(on, half), hs[:, 3, part].unsqueeze(2).broadcast_to([P, 2 * H, DH]), ALU.subtract).then_inc(o_cent, 1)

            def variance(half):
                dve.wait_ge(o_sq, half + 1)
                V.tensor_reduce(hs[:, 1, 2 * H * half:2 * H * (half + 1)], heads(big, half), AX.X, ALU.add).then_inc(gn_var, 1)

            def gate(half):
                part = slice(2 * H * half, 2 * H * (half + 1))
                tl = slice(2 * half, 2 * half + 2)
                dve.wait_ge(gn_r, half + 1)
                then(V.tensor_tensor(heads(on, half), heads(on, half), hs[:, 2, part].unsqueeze(2).broadcast_to([P, 2 * H, DH]), ALU.mult))
                dve.wait_ge(gain_ready, half + 1)
                then(V.tensor_tensor(on[:, tl, :], on[:, tl, :], sg[:, tl, :], ALU.mult))
                V.tensor_tensor(on[:, tl, :], on[:, tl, :], sgb[:, tl, :], ALU.add).then_inc(o_gated, 1)

            def residual_mixer(half):
                tl = slice(2 * half, 2 * half + 2)
                dve.wait_ge(res_mm, 3 + half)
                V.tensor_tensor(acc[:, tl, :], X[:, tl, :], ps[2 + half][:].rearrange("p (i d) -> p i d", i=2), ALU.add).then_inc(res_add, 1)
                dve.wait_ge(res_add, 3 + half)
                norm_tokens(4 + half, acc, big)

            dve.wait_ge(a_zero, 1)
            dve.wait_ge(v_evac, 2)
            dve.wait_ge(vec, 1)
            for k in range(5):
                pick_weights(k)
            centre(0)
            pick_weights(5)
            variance(0)
            pick_weights(6)
            gate(0)
            pick_weights(7)
            centre(1)
            variance(1)
            gate(1)
            residual_mixer(0)
            residual_mixer(1)

            F = lambda k: fe[:, k]
            flat = lambda k: fe[:, k].rearrange("p i e -> p (i e)")
            dve.wait_ge(gate_exp, 1)
            then(V.tensor_scalar(flat(1), flat(0), 1.0, None, ALU.add))
            then(V.reciprocal(flat(2), flat(1)))
            then(V.tensor_tensor(F(3), F(2), ebias[:].unsqueeze(1).broadcast_to([P, NT, NE]), ALU.add))
            q4 = flat(3).rearrange("p (g e) -> p g e", e=4)
            G = lambda k: fg[:, k].rearrange("p i g -> p (i g)").unsqueeze(2)
            V.tensor_tensor(G(0), q4[:, :, 0:1], q4[:, :, 1:2], ALU.max)
            V.tensor_tensor(G(1), q4[:, :, 0:1], q4[:, :, 1:2], ALU.min)
            V.tensor_tensor(G(2), q4[:, :, 2:3], q4[:, :, 3:4], ALU.max)
            then(V.tensor_tensor(G(3), q4[:, :, 2:3], q4[:, :, 3:4], ALU.min))
            V.tensor_tensor(G(4), G(0), G(2), ALU.max)
            V.tensor_tensor(G(5), G(0), G(2), ALU.min)
            then(V.tensor_tensor(G(6), G(1), G(3), ALU.max))
            then(V.tensor_tensor(G(5), G(5), G(6), ALU.max))
            then(V.tensor_tensor(G(7), G(4), G(5), ALU.add))

            def ranks(src, n, table, w_, dst):
                other = src.unsqueeze(2).broadcast_to([P, NT, n, n])
                own = src.unsqueeze(3).broadcast_to([P, NT, n, n])
                V.tensor_tensor(w_[0], other, own, ALU.is_gt)
                then(V.tensor_tensor(w_[1], other, own, ALU.is_equal))
                m_ = lambda k: w_[k].rearrange("p i a b -> p i (a b)")
                then(V.tensor_tensor(m_(1), m_(1), table.unsqueeze(1).broadcast_to([P, NT, n * n]), ALU.mult))
                then(V.tensor_tensor(m_(1), m_(1), m_(0), ALU.add))
                then(V.tensor_reduce(dst, w_[1].rearrange("p i a b -> p (i a) b"), AX.X, ALU.add))

            gwv = [gw[:, k].rearrange("p i (a b) -> p i a b", a=4) for k in range(2)]
            ranks(fg[:, 7], NGRP, gbefore[:], gwv, fg[:, 0].rearrange("p i g -> p (i g)"))
            then(V.tensor_scalar(fg[:, 1].rearrange("p i g -> p (i g)"), fg[:, 0].rearrange("p i g -> p (i g)"), float(TOPG), None, ALU.is_lt))
            then(V.tensor_tensor(flat(4).rearrange("p (g e) -> p g e", e=4), q4, G(1).broadcast_to([P, NT * NGRP, 4]), ALU.mult))
            ranks(F(4), NE, before[:], pw, flat(5))
            then(V.scalar_tensor_tensor(flat(6), flat(5), float(TOPK), flat(2), ALU.is_lt, ALU.mult))
            then(V.tensor_reduce(hs[:, 0, 0:NT], F(6), AX.X, ALU.add))
            then(V.tensor_scalar(hs[:, 0, 4:4 + NT], hs[:, 0, 0:NT], 1e-20, None, ALU.add))
            then(V.reciprocal(hs[:, 0, 8:8 + NT], hs[:, 0, 4:4 + NT]))
            then(V.tensor_scalar(hs[:, 0, 12:12 + NT], hs[:, 0, 8:8 + NT], 2.5, None, ALU.mult))
            then(V.tensor_tensor(F(7), F(6), hs[:, 0, 12:12 + NT].unsqueeze(2).broadcast_to([P, NT, NE]), ALU.mult))

            def gated(e):
                dve.wait_ge(silu, e + 1)
                dve.wait_ge(gu_mm, 2 * e + 2)
                if e >= 2:
                    dve.wait_ge(down_mm, 2 * (e - 1))
                V.tensor_tensor(inter[e % 2][:], sil[e % 2][:], ps[2 * (e % 2) + 1][:], ALU.mult).then_inc(inter_ready, 1)

            def accumulate(e):
                for i in range(NT):
                    dve.wait_ge(down_mm, 2 * e + i // 2 + 1)
                    if e >= 1:
                        dve.wait_ge(acc_done, NT * (e - 1) + i + 1)
                    y = ps[4 + 2 * (e % 2) + i // 2][:, (i % 2) * D:(i % 2 + 1) * D]
                    if e < NE:
                        V.scalar_tensor_tensor(acc[:, i, :], y, fe[:, 7, i, e:e + 1], acc[:, i, :], ALU.mult, ALU.add).then_inc(acc_done, 1)
                    else:
                        V.tensor_tensor(acc[:, i, :], acc[:, i, :], y, ALU.add).then_inc(acc_done, 1)

            for e in range(NE + 1):
                gated(e)
                if e >= 1:
                    accumulate(e - 1)
            accumulate(NE)


def kernel(**inputs):
    import concourse.bacc as _bacc
    from concourse.bass_utils import run_bass_kernel_spmd as _run

    f = {k: np.ascontiguousarray(v) for k, v in inputs.items()}
    arrays = {k: f[k] for k in ("x", "ctx_768", "L0_xattn_bo", "L0_attn_b_w2", "L0_attn_gn_weight", "L0_attn_gn_bias", "L0_ffn_e_bias")}
    halves = lambda k, n: f[k].reshape(2, n).T
    twice = lambda k: np.concatenate([f[k], f[k]])[:, None]
    arrays["v_lnx"] = np.ascontiguousarray(np.concatenate([halves("L0_xattn_ln_x_g", HALF), halves("L0_xattn_ln_x_b", HALF)], axis=1))
    arrays["v_cols"] = np.ascontiguousarray(np.concatenate(
        [halves("L0_xattn_ln_l_g", P), halves("L0_xattn_ln_l_b", P), halves("L0_attn_mu0", P), f["L0_attn_bonus"].reshape(P, 1),
         twice("L0_xattn_qn_g"), twice("L0_xattn_kn_g"), f["L0_attn_x_bias"].reshape(5, 2, P).transpose(2, 1, 0).reshape(P, 10)], axis=1))
    for k, src in (("t_Wkv", "L0_xattn_Wkv"), ("t_Wq", "L0_xattn_Wq"), ("t_Wlkv", "L0_xattn_Wlkv"), ("t_Wo", "L0_xattn_Wo"),
                   ("t_W_x0", "L0_attn_W_x0"), ("t_W_x2", "L0_attn_W_x2"), ("t_W_r", "L0_attn_W_r"),
                   ("t_W_k", "L0_attn_W_k"), ("t_W_w1", "L0_attn_W_w1"), ("t_W_w2", "L0_attn_W_w2"), ("t_W_v", "L0_attn_W_v"),
                   ("t_W_g", "L0_attn_W_g"), ("t_W_o", "L0_attn_W_o"), ("t_gate_w", "L0_ffn_gate_w"), ("t_shared_gate", "L0_ffn_shared_gate_w"),
                   ("t_shared_up", "L0_ffn_shared_up_w"), ("t_shared_down", "L0_ffn_shared_down_w")):
        arrays[k] = np.ascontiguousarray(f[src].T)
    for k, src in (("t_gate_proj", "L0_ffn_gate_proj"), ("t_up_proj", "L0_ffn_up_proj"), ("t_down_proj", "L0_ffn_down_proj")):
        arrays[k] = np.ascontiguousarray(f[src].transpose(0, 2, 1))
    mask = f["mask_BxS2_bk0"].astype(np.int32)
    lead = mask[:, 0:FULL * P].reshape(B, P, FULL).transpose(0, 2, 1).reshape(B, FULL * P)
    arrays["p_mask"] = np.ascontiguousarray(np.concatenate([lead, mask[:, FULL * P:], np.ones((B, MROW - S), np.int32)], axis=1).reshape(P, MPIECE))
    arrays.update(constants())

    nc = _bacc.Bacc("TRN2", target_bir_lowering=False, num_devices=1)
    aps = {k: nc.dram_tensor(f"in_{k}", v.shape, mybir.dt.from_np(v.dtype), kind="ExternalInput").ap() for k, v in arrays.items()}
    out = nc.dram_tensor("out_0", (B, T, D), F32, kind="ExternalOutput").ap()
    build(nc, aps, out)
    r = _run(nc, [{f"in_{k}": v for k, v in arrays.items()}], core_ids=[0])
    return r.results[0]["out_0"]
```

```python
from contextlib import ExitStack

import numpy as np

import concourse.bass as bass
from concourse import mybir

F32 = mybir.dt.float32
F32R = mybir.dt.float32r
BF16 = mybir.dt.bfloat16
U8 = mybir.dt.uint8
I32 = mybir.dt.int32
ALU = mybir.AluOpType
ACT = mybir.ActivationFunctionType
AX = mybir.AxisListType

P = 128
B, T, D = 8, 64, 256
S, DC = 1601, 192
H, DH = 4, 64
NT = B * T // P
HALF = DC // 2
W = HALF + 1
ROW = 2 * W
MROW = 1680
MPIECE = B * MROW // P
LOWEST = -3e38
FULL = S // P
TAIL = S - FULL * P
NG = (FULL + 1) // 2 + 1
KEYS = S + T
NPAIR = H // 2
CH = 512
NCH = -(-KEYS // CH)
STEPS = NPAIR * NCH
NE, INTER, TOPK, TOPG, NGRP = 16, 128, 4, 2, 4
LEVELS = 6
LN_EPS = 1e-5
MASKED = -1e30
ARENA = 28928
NXH = 4


def constants():
    i = np.arange(P)
    same = i[:, None] // T == i[None, :] // T
    u, pos = i[:, None], i[None, :]
    sums = np.zeros((P, LEVELS, P), np.float32)
    pick = np.zeros((P, LEVELS, P // 2), np.int32)
    for lv in range(LEVELS):
        m = 1 << lv
        right = (pos // m) % 2 == 1
        sums[:, lv] = same & (u // m == pos // m) & np.where(right, u < pos, u > pos)
        queries = pos[:, right[0]]
        pick[:, lv] = (u // T == queries // T) & (u // (2 * m) == queries // (2 * m)) & ((u // m) % 2 == 0)
    e = np.arange(NE)
    return {
        "c_ident": np.eye(P, dtype=np.float32),
        "c_sums": sums,
        "c_pick": pick,
        "c_head": (i[:, None] // 32 == np.arange(4)[None, :]).astype(np.float32),
        "c_before": (e[None, :] < e[:, None]).astype(np.float32).reshape(1, NE * NE),
        "c_gbefore": (np.arange(4)[None, :] < np.arange(4)[:, None]).astype(np.float32).reshape(1, 16),
    }


def build(nc, a, out):
    x_dram = a["x"].rearrange("b t d -> (b t) d").rearrange("(i p) d -> p i d", p=P)
    out_dram = out.rearrange("b t d -> (b t) d").rearrange("(i p) d -> p i d", p=P)
    with ExitStack() as ctx:
        def sb(name, shape, dt=F32):
            return ctx.enter_context(nc.sbuf_tensor(name, shape, dt))

        def sem(name):
            return ctx.enter_context(nc.semaphore(name))

        ps = [ctx.enter_context(nc.psum_tensor(f"bank{i}", [P, 512], F32)) for i in range(8)]
        score_bank, k_bank, tx_bank, tp_bank, y_bank = ps[0:4], ps[4], ps[5], ps[6], ps[7]

        arena = sb("arena", [P, ARENA])

        def carve(at, *shapes):
            views = []
            for shape in shapes:
                n = int(np.prod(shape[1:]))
                v = arena[0:shape[0], at:at + n]
                if len(shape) == 3:
                    v = v.rearrange("p (a b) -> p a b", a=shape[1])
                if len(shape) == 4:
                    v = v.rearrange("p (a b c) -> p a b c", a=shape[1], b=shape[2])
                views.append(v)
                at += n
            assert at <= ARENA, at
            return (*views, at)

        ident = sb("ident", [P, P])
        sums = sb("sums", [P, LEVELS, P])
        pick = sb("pick", [P, LEVELS, P // 2], I32)
        headsel = sb("headsel", [P, 4])
        split_a = sb("split_a", [P, 6, 2, D], F32R)
        split_b = sb("split_b", [P, 6, B * T], F32R)
        wkh, wkl = split_a[0:W, 0], split_a[0:W, 1]
        xhT = [split_a[0:W, 2 + i] for i in range(2)]
        xhTl = [split_a[0:W, 4 + i] for i in range(2)]
        gu_part = [[split_a[:, 2 * i + part] for part in range(2)] for i in range(2)]
        down_part = [[split_a[:, 4 + i, part] for part in range(2)] for i in range(2)]
        x_part = [split_b[:, 2 * part:2 * part + 2] for part in range(2)]
        inter_part = [split_b[:, 4 + part] for part in range(2)]
        before = sb("before", [P, NE * NE])
        gbefore = sb("gbefore", [P, 16])
        neg_half = sb("neg_half", [P, 64])
        ones_row = sb("ones_row", [1, P])
        wkv = sb("wkv", [W, 2, 2 * D])
        lnx = sb("lnx", [HALF, 4])
        lnx_g, lnx_b = lnx[:, 0:2], lnx[:, 2:4]
        cols = sb("cols", [P, 19])
        lnl_g, lnl_b, mu0, bonus, qg, kg = (cols[:, i:j] for i, j in ((0, 2), (2, 4), (4, 6), (6, 7), (7, 8), (8, 9)))
        xbias = cols[:, 9:19].rearrange("p (c i) -> p c i", c=2)
        qkg = sb("qkg", [P, 1])
        wo = sb("wo", [P, 2, D])
        bo = sb("bo", [1, D])
        wx0 = sb("wx0", [P, 2, 160])
        wx2b = sb("wx2b", [32, D])
        wr = sb("wr", [P, 2, 128])
        wk = sb("wk", [P, 2, 128])
        ww1 = sb("ww1", [P, 2, 64])
        ww2 = sb("ww2", [65, 128])
        wv = sb("wv", [P, 2, D])
        wg = sb("wg", [P, 2, D])
        wo2 = sb("wo2", [P, 2, D])
        gnw = sb("gnw", [P, D])
        gnb = sb("gnb", [P, D])
        gatew = sb("gatew", [P, 2, NE])
        ebias = sb("ebias", [P, NE])
        mask_flat = sb("mask_flat", [P, MPIECE], BF16)
        mask_row = sb("mask_row", [P, 2, MROW], BF16)
        mask_bc = [sb(f"mask_bc{i}", [P, MROW], BF16) for i in range(2)]
        mask_in = mask_bc[1].bitcast(I32)[:, 0:MPIECE]

        wx2a = mask_row[:].rearrange("p a m -> p (a m)").bitcast(F32)[:, 0:4 * D].rearrange("p (i d) -> p i d", i=4)

        X = sb("X", [P, NT, D])
        big = sb("big", [P, NT, D])
        st = sb("st", [P, NT, 6])
        mv = sb("mv", [P, NT, 2])
        rs = sb("rs", [P, NT])
        xT = sb("xT", [P, 2, B * T])
        qkss = sb("qkss", [P, 2 * NT * H])
        qkr = sb("qkr", [P, 2 * NT * H])
        oT = sb("oT", [P, NPAIR, B * T])
        oT2 = oT

        *xh, at = carve(0, *[(P, FULL + 1, ROW)] * NXH)
        at_kT1 = at + NPAIR * S
        *kT, at = carve(at, *[(P, NPAIR, S)] * 2)
        *pr, at = carve(at, *[(P, KEYS)] * 2)
        *pT, at = carve(at, *[(P, 4, P)] * 2)
        *kn, at = carve(at, *[(P, 512)] * 2)
        *kraw, at = carve(at, *[(P, 512)] * 2)
        xn, wkv_raw, _ = carve(at_kT1, (P, NT, D), (HALF, 2, 2 * D))
        qk, _ = carve(at_kT1, (P, 2, NT, D))
        wq, wlkv, _ = carve(3 * (FULL + 1) * ROW, (P, 2, D), (P, 2, 2 * D))
        ksq, qb, klT, vlat, at = carve(at, (P, 512), (P, B * NPAIR, P), (P, NPAIR, B * T), (T, B, D))
        cst = sb("cst", [P, 2, 2, 6])
        cmv = sb("cmv", [P, 2, 2, 2])
        crs = sb("crs", [P, 2, 2])
        kss = sb("kss", [P, 2, 8])
        kr = sb("kr", [P, 2, 8])
        mx = sb("mx", [P, 2, NCH])
        nm = sb("nm", [P, 2])
        ls = sb("ls", [P, 2, NCH])
        lsum = sb("lsum", [P, 2])
        rl = sb("rl", [P, 2])
        plat = sb("plat", [P, T])
        plT = sb("plT", [T, P])
        ysb = sb("ysb", [P, 2 * W])
        yT = sb("yT", [W, 2, P])

        experts, at = carve(0, (P, NE + 1, 3 * 2 * INTER))
        ed = experts[:, :, 4 * INTER:]
        delta, at = carve(at, (P, 2, B * T))
        at_mixed = at
        *mixed, at_tmix = carve(at, *[(P, 2, B * T)] * 5)
        aT, sgb, _ = carve(at_mixed, (P, NT, H, P), (P, NT, D))
        sil0, sil1, inter0, inter1, at_pw = carve(at_mixed, *[(P, B * T)] * 4)
        sil, inter = [sil0, sil1], [inter0, inter1]
        pw, _ = carve(at_pw, (P, 2, NT * NE * NE))
        pw = [pw[:, k].rearrange("p (i a b) -> p i a b", i=NT, a=NE) for k in range(2)]
        *tmix, at = carve(at_tmix, *[(P, B * T)] * 2)
        on, _ = carve(at_tmix - 2 * 2 * B * T, (P, NT, D))
        rblk1, _ = carve(at_tmix, (P, NT, H, P // 2))
        xpa, rT, rkT, ew, vn, sg, ex, ruk, rblk0, at = carve(
            at, (P, B * T), (P, B * T), (P, B * T), (P, NT, 128), (P, NT, D), (P, NT, D), (P, LEVELS, B * T), (P, B * T), (P, NT, H, P // 2))
        rblk = [rblk0, rblk1]
        acc = ex[:, 0:2, :].rearrange("p a (i d) -> p (a i) d", d=D)
        xpb = sb("xpb", [32, B * T])
        wt = sb("wt", [65, B * T])
        dcoef = sb("dcoef", [P, NT, 4])
        hs = sb("hs", [P, 4, NT * H])
        fe = sb("fe", [P, 12, NT, NE])
        fg = sb("fg", [P, 8, NT, NGRP])
        gw = sb("gw", [P, 3, NT, 16])

        x_in = sem("x_in"); ctx_first = sem("ctx_first"); lat_in = sem("lat_in"); setup_in = sem("setup_in"); mixer_in = sem("mixer_in"); expert_in = sem("expert_in")
        ctx_in = [sem(f"ctx_in{i}") for i in range(2)]; mask_in_sem = sem("mask_in_sem")
        stored = sem("stored")
        pool_const = sem("pool_const"); mask_ready = sem("mask_ready"); mask_rows = sem("mask_rows"); mask_spread = sem("mask_spread"); wk_split = sem("wk_split")
        ln_stats = sem("ln_stats"); ln_aggr = sem("ln_aggr"); ln_rstd = sem("ln_rstd"); ln_out = sem("ln_out")
        tok_T = sem("tok_T"); tok_T_evac = sem("tok_T_evac")
        wkv_bias = sem("wkv_bias"); wkv_ready = sem("wkv_ready")
        lat_mm = sem("lat_mm")
        vlat_mm = sem("vlat_mm"); vlat_evac = sem("vlat_evac")
        lat_sq = sem("lat_sq"); lat_ss = sem("lat_ss"); lat_r = sem("lat_r"); lat_n = sem("lat_n")
        lat_nT = sem("lat_nT"); lat_nT_evac = sem("lat_nT_evac"); lat_kT_evac = sem("lat_kT_evac")
        cstat = sem("cstat"); caggr = sem("caggr"); crstd = sem("crstd"); xh_ready = sem("xh_ready")
        xhT_mm = sem("xhT_mm"); xhT_evac = sem("xhT_evac"); xhT_low = sem("xhT_low")
        k_mm = sem("k_mm"); k_sq = sem("k_sq"); k_evac = sem("k_evac"); k_ss = sem("k_ss"); k_r = sem("k_r"); k_n = sem("k_n")
        kT_mm = sem("kT_mm"); kT_evac = sem("kT_evac")
        score_mm = sem("score_mm"); chunk_max = sem("chunk_max"); row_max = sem("row_max")
        exp_done = sem("exp_done"); row_sum = sem("row_sum"); row_inv = sem("row_inv"); plat_ready = sem("plat_ready")
        pT_mm = sem("pT_mm"); pT_evac = sem("pT_evac"); y_mm = sem("y_mm"); y_evac = sem("y_evac")
        yT_mm = sem("yT_mm"); yT_evac = sem("yT_evac"); o_mm = sem("o_mm"); o_evac = sem("o_evac")
        res_mm = sem("res_mm"); res_add = sem("res_add")
        d_ready = sem("d_ready"); xx_ready = sem("xx_ready"); xp_mm = sem("xp_mm"); xp_act = sem("xp_act")
        wx2_zero = sem("wx2_zero"); wx2_in = sem("wx2_in"); mu_mm = sem("mu_mm"); mu_use = sem("mu_use"); mixed_even = sem("mixed_even"); mixed_odd = sem("mixed_odd")
        r_mm = sem("r_mm"); r_evac = sem("r_evac"); kk_mm = sem("kk_mm"); kk_evac = sem("kk_evac")
        w1_mm = sem("w1_mm"); w1_act = sem("w1_act"); w2_mm = sem("w2_mm"); w2_act = sem("w2_act")
        v_mm = sem("v_mm"); v_evac = sem("v_evac"); g_mm = sem("g_mm"); g_act = sem("g_act")
        e_mm = sem("e_mm"); e_act = sem("e_act"); ruk_ready = sem("ruk_ready"); dc_mm = sem("dc_mm")
        left_ready = sem("left_ready"); right_ready = sem("right_ready"); r_zero = sem("r_zero"); a_first = sem("a_first"); a_last = sem("a_last"); v_centred = sem("v_centred"); a_mm = sem("a_mm"); a_pick = sem("a_pick")
        av_mm = sem("av_mm"); vec = sem("vec"); o_gain = sem("o_gain"); o_sq = sem("o_sq")
        gn_var = sem("gn_var"); gn_r = sem("gn_r"); gain_ready = sem("gain_ready"); o_gated = sem("o_gated"); oT2_mm = sem("oT2_mm"); oT2_evac = sem("oT2_evac")
        gu_high = sem("gu_high"); gu_low = sem("gu_low"); ed_high = sem("ed_high"); ed_low = sem("ed_low")
        x_high = sem("x_high"); x_low = sem("x_low"); inter_high = sem("inter_high"); inter_low = sem("inter_low")
        gate_mm = sem("gate_mm"); gate_exp = sem("gate_exp")
        gu_mm = sem("gu_mm"); silu = sem("silu"); inter_ready = sem("inter_ready"); down_mm = sem("down_mm"); acc_done = sem("acc_done")
        pool_tick = sem("pool_tick"); vec_tick = sem("vec_tick")

        def rows(t):
            return P if t < FULL else TAIL

        def tiles(g):
            return [2 * g, 2 * g + 1] if 2 * g + 1 < FULL else [2 * g]

        groups = B * NG
        chunks = B * STEPS
        steps = (B + 2) * STEPS

        def group_of(u):
            b, k = divmod(u, STEPS)
            return b * NG + k if b < B and k < NG else None

        def chunk_of(u):
            m = u - STEPS
            return m if 0 <= m < chunks else None

        def lag(u, n):
            return chunk_of(u - n) if u >= n else None

        def span(c):
            return c * CH, min(KEYS, (c + 1) * CH)

        def key_tiles(c):
            return [(t, t * P, t * P + rows(t)) for t in range(4 * c, min(4 * c + 4, FULL + 1))]

        block = ctx.enter_context(nc.Block())

        LATENT_BANK = (2, 3, 6, 7)

        ORDER = [1, 0, 2, 3, 4]
        NORMS = [(0, NT), (0, NT), (0, 2), (2, 4), (0, 2), (2, 4)]

        def normed(n):
            return sum(hi - lo for lo, hi in NORMS[:n + 1])

        def kn_sq(i):
            return pr[i // 2][:, (i % 2) * 512:(i % 2 + 1) * 512]

        @block.sync
        def _(sp):
            first = a["ctx_768"][0, 0:FULL * P, :].rearrange("(p t) d -> p t d", t=FULL)[:, 0:4, :]
            sp.dma_start(xh[0][:, 0:4, 0:DC], first).then_inc(ctx_first, 16)
            for dst, src in (
                (ident[:], a["c_ident"]), (cols[:], a["v_cols"]), (lnx[:], a["v_lnx"]),
                (wkv_raw[:], a["t_Wkv"].rearrange("(c p) n -> p c n", p=HALF)),
            ):
                sp.dma_start(dst, src).then_inc(setup_in, 16)
            for b in range(B):
                if b >= 2:
                    sp.wait_ge(ctx_in[b % 2], 32 * (b // 2))
                if b >= NXH:
                    sp.wait_ge(y_mm, NPAIR * (b - NXH + 1))
                if b == 3:
                    sp.wait_ge(vlat_mm, 4)
                buf = xh[b % NXH]
                full = a["ctx_768"][b, 0:FULL * P, :].rearrange("(p t) d -> p t d", t=FULL)
                if b == 0:
                    sp.dma_start(X[:], x_dram).then_inc(x_in, 16)
                    sp.dma_start(buf[:, 4:FULL, 0:DC], full[:, 4:FULL, :]).then_inc(ctx_in[0], 16)
                else:
                    sp.dma_start(buf[:, 0:FULL, 0:DC], full).then_inc(ctx_in[b % 2], 16)
                sp.dma_start(buf[0:TAIL, FULL, 0:DC], a["ctx_768"][b, FULL * P:S, :]).then_inc(ctx_in[b % 2], 16)
                if b == 0:
                    sp.dma_start(wq[:], a["t_Wq"].rearrange("(c p) n -> p c n", p=P)).then_inc(lat_in, 16)
                    sp.dma_start(wlkv[:], a["t_Wlkv"].rearrange("(c p) n -> p c n", p=P)).then_inc(lat_in, 16)
                    sp.dma_start(mask_in, a["p_mask"]).then_inc(mask_in_sem, 16)
                if b == 1:
                    sp.wait_ge(mask_ready, 1)
                    for k in range(B):
                        sp.dma_start(mask_row[32 * (k % 4):32 * (k % 4) + 1, k // 4, :].rearrange("o (p m) -> o p m", m=MPIECE),
                                     mask_flat[k * P // B:(k + 1) * P // B, :]).then_inc(mask_rows, 16)
                    for dst, src in (
                        (wo[:], a["t_Wo"].rearrange("(c p) n -> p c n", p=P)),
                        (bo[:], a["L0_xattn_bo"].rearrange("(o d) -> o d", o=1)),
                        (sums[:], a["c_sums"]), (pick[:], a["c_pick"]), (headsel[:], a["c_head"]),
                        (wx0[:], a["t_W_x0"].rearrange("(c p) n -> p c n", p=P)),
                        (wx2b[:], a["t_W_x2"][P:160, :]),
                        (wr[:], a["t_W_r"].rearrange("(c p) n -> p c n", p=P)),
                        (wk[:], a["t_W_k"].rearrange("(c p) n -> p c n", p=P)),
                        (ww1[:], a["t_W_w1"].rearrange("(c p) n -> p c n", p=P)),
                        (ww2[0:64, :], a["t_W_w2"]), (ww2[64:65, :], a["L0_attn_b_w2"].rearrange("(o d) -> o d", o=1)),
                        (wv[:], a["t_W_v"].rearrange("(c p) n -> p c n", p=P)),
                        (wg[:], a["t_W_g"].rearrange("(c p) n -> p c n", p=P)),
                        (wo2[:], a["t_W_o"].rearrange("(c p) n -> p c n", p=P)),
                        (gnw[:], a["L0_attn_gn_weight"].rearrange("(o d) -> o d", o=1).broadcast_to([P, D])),
                        (gnb[:], a["L0_attn_gn_bias"].rearrange("(o d) -> o d", o=1).broadcast_to([P, D])),
                        (gatew[:], a["t_gate_w"].rearrange("(c p) n -> p c n", p=P)),
                        (ebias[:], a["L0_ffn_e_bias"].rearrange("(o d) -> o d", o=1).broadcast_to([P, NE])),
                        (before[:], a["c_before"].broadcast_to([P, NE * NE])),
                        (gbefore[:], a["c_gbefore"].broadcast_to([P, 16])),
                    ):
                        sp.dma_start(dst, src).then_inc(mixer_in, 16)
            sp.wait_ge(wx2_zero, 1)
            for i in range(4):
                sp.dma_start(wx2a[32 * i:32 * i + 32, i, :], a["t_W_x2"][32 * i:32 * i + 32, :]).then_inc(wx2_in, 16)
            sp.wait_ge(o_evac, 2 * NPAIR * B)
            sp.wait_ge(pT_evac, B * STEPS)
            for lo, hi in ((0, 4), (4, 10), (10, NE + 1)):
                sp.dma_start(experts[:, lo:hi], a["p_experts"][lo:hi].rearrange("e p n -> p e n")).then_inc(expert_in, 16)
            for i in range(NT):
                sp.wait_ge(acc_done, NE * NT + i + 1)
                sp.dma_start(out_dram[:, i, :], acc[:, i, :]).then_inc(stored, 16)
            sp.wait_ge(stored, 16 * NT)

        SETUP = 4 * 16
        LATENT = 2 * 16
        MIXER = 21 * 16
        EXPERT = 3 * 16

        @block.gpsimd
        def _(pool):
            tick = [0]

            def then(ins):
                tick[0] += 1
                ins.then_inc(pool_tick, 1)
                pool.wait_ge(pool_tick, tick[0])

            then(pool.memset(neg_half[:], -0.5))
            then(pool.memset(ones_row[:], 1.0))
            then(pool.memset(wt[64:65, :], 1.0))
            for i in range(NXH - 1):
                then(pool.memset(xh[i][:, :, DC:DC + 1], 1.0))
            pool.memset(qb[:], 0.0).then_inc(pool_const, 1)
            pool.wait_ge(pool_const, 1)

            def rstd(n):
                lo, hi = NORMS[n]
                pool.wait_ge(ln_aggr, n + 1)
                then(pool.tensor_scalar(rs[:, lo:hi], mv[:, lo:hi, 1], LN_EPS, None, ALU.add))
                pool.tensor_tensor(rs[:, lo:hi], rs[:, lo:hi], neg_half[:, 0:hi - lo], ALU.pow).then_inc(ln_rstd, 1)

            def group_rstd(n):
                pool.wait_ge(caggr, n + 1)
                k, r = len(tiles(n % NG)), rows(tiles(n % NG)[0])
                then(pool.tensor_scalar(crs[0:r, n % 2, 0:k], cmv[0:r, n % 2, 0:k, 1], LN_EPS, None, ALU.add))
                pool.tensor_tensor(crs[0:r, n % 2, 0:k], crs[0:r, n % 2, 0:k], neg_half[0:r, 0:k], ALU.pow).then_inc(crstd, 1)

            group_rstd(0)
            group_rstd(1)

            def spread_mask(b):
                pool.wait_ge(k_r, b * NG + (2 if b else NG))
                if b == 0:
                    pool.wait_ge(mask_rows, 16 * B)
                if b >= 2:
                    pool.wait_ge(chunk_max, STEPS * (b - 1))
                pool.partition_broadcast(mask_bc[b % 2][:], mask_row[32 * (b % 4):32 * (b % 4) + 1, b // 4, :]).then_inc(mask_spread, 1)
                pool.wait_ge(mask_spread, b + 1)

            def mask_bias():
                pool.wait_ge(mask_in_sem, 16)
                pool.tensor_scalar(mask_flat[:], mask_in, 1.0, -MASKED, ALU.subtract, ALU.mult).then_inc(mask_ready, 1)
                pool.wait_ge(mask_ready, 1)

            def latent_rms(half):
                pool.wait_ge(lat_ss, 4 * (half + 1))
                of_half = lambda v: v[:].rearrange("p (j x) -> p j x", j=2)[:, :, 2 * H * half:2 * H * (half + 1)]
                then(pool.tensor_scalar(of_half(qkr), of_half(qkss), 1.0 / DH, 1e-16, ALU.mult, ALU.max))
                pool.tensor_tensor(of_half(qkr), of_half(qkr), neg_half[:, 0:4 * H].rearrange("p (j x) -> p j x", j=2), ALU.pow).then_inc(lat_r, 1)

            for u in range(steps):
                n = group_of(u)
                if u == STEPS:
                    pool.wait_ge(vlat_mm, 4)
                    then(pool.memset(xh[3][:, :, DC:DC + 1], 1.0))
                if u % STEPS == (2 if u >= STEPS else STEPS - 1) and u // STEPS < B:
                    spread_mask(u // STEPS)
                if n is None:
                    continue
                if n + 2 < groups:
                    group_rstd(n + 2)
                pool.wait_ge(k_ss, n + 1)
                k, r = 4 * len(tiles(n % NG)), rows(tiles(n % NG)[0])
                then(pool.tensor_scalar(kr[0:r, n % 2, 0:k], kss[0:r, n % 2, 0:k], 1.0 / DH, 1e-16, ALU.mult, ALU.max))
                pool.tensor_tensor(kr[0:r, n % 2, 0:k], kr[0:r, n % 2, 0:k], neg_half[0:r, 0:k], ALU.pow).then_inc(k_r, 1)
                if u == STEPS * B - 4:
                    pool.memset(wx2a, 0.0).then_inc(wx2_zero, 1)
                    pool.wait_ge(wx2_zero, 1)
                if u == 0:
                    rstd(0)
                if u == 1:
                    rstd(1)
                if u == 2:
                    mask_bias()
                if u in (4, 6):
                    latent_rms((u - 4) // 2)
            rstd(2)
            rstd(3)
            pool.wait_ge(o_evac, 2 * NPAIR * B)
            pool.memset(rblk[0], 0.0).then_inc(r_zero, 1)
            pool.wait_ge(r_zero, 1)
            for k, i in enumerate(ORDER):
                pool.wait_ge(mu_use, 2 * k + 2)
                pool.tensor_tensor(mixed[i][:, 1, :], tmix[1][:], xT[:, 1, :], ALU.add).then_inc(mixed_odd, 1)
                pool.wait_ge(mixed_odd, k + 1)
            pool.wait_ge(mixed_even, 5)
            pool.memset(rblk[1], 0.0).then_inc(r_zero, 1)
            pool.wait_ge(r_zero, 2)
            pool.wait_ge(kk_evac, 1)
            for lv in range(LEVELS):
                if lv % 3 == 0:
                    pool.wait_ge(e_act, NT * (lv // 3 + 1))
                left = lambda v: v.rearrange("p (n s m) -> p n s m", s=2, m=1 << lv)[:, :, 0]
                pool.tensor_tensor(left(ex[:, lv, :]), left(ex[:, lv, :]), left(rkT), ALU.mult).then_inc(left_ready, 1)
                pool.wait_ge(left_ready, lv + 1)
            pool.wait_ge(vec, 1)
            pool.wait_ge(r_mm, 1)
            pool.wait_ge(w1_mm, 1)
            pool.tensor_tensor(aT[:, 0:2].rearrange("p i h t -> p (i h) t"), ident[:].unsqueeze(1).broadcast_to([P, 2 * H, P]),
                               dcoef[:, 0:2, :].rearrange("p i h -> p (i h)").unsqueeze(2).broadcast_to([P, 2 * H, P]), ALU.mult).then_inc(a_first, 1)
            pool.wait_ge(a_first, 1)
            for h in range(2):
                pool.wait_ge(g_act, h + 1)
                tl = slice(2 * h, 2 * h + 2)
                then(pool.tensor_tensor(sgb[:, tl, :], sg[:, tl, :], gnb[:].unsqueeze(1).broadcast_to([P, 2, D]), ALU.mult))
                pool.tensor_tensor(sg[:, tl, :], sg[:, tl, :], gnw[:].unsqueeze(1).broadcast_to([P, 2, D]), ALU.mult).then_inc(gain_ready, 1)
                pool.wait_ge(gain_ready, h + 1)

            def gate_up_low(e):
                pool.wait_ge(gu_high, e + 1)
                pool.tensor_tensor(gu_part[e % 2][1].rearrange("p a b -> p (a b)"), experts[:, e, 0:512], gu_part[e % 2][0].rearrange("p a b -> p (a b)").bitcast(F32), ALU.subtract).then_inc(gu_low, 1)

            def down_low(e):
                pool.wait_ge(ed_high, e + 1)
                pool.tensor_tensor(down_part[e % 2][1], ed[:, e, :], down_part[e % 2][0].bitcast(F32), ALU.subtract).then_inc(ed_low, 1)

            gate_up_low(0)
            gate_up_low(1)
            down_low(0)
            for h in range(2):
                pool.wait_ge(gn_var, h + 1)
                part = slice(2 * H * h, 2 * H * (h + 1))
                then(pool.tensor_scalar(hs[:, 2, part], hs[:, 1, part], 1.0 / DH, LN_EPS, ALU.mult, ALU.add))
                pool.tensor_tensor(hs[:, 2, part], hs[:, 2, part], neg_half[:, 0:2 * H], ALU.pow).then_inc(gn_r, 1)
            rstd(4)
            rstd(5)
            for e in range(NE + 1):
                if e + 2 < NE + 1:
                    gate_up_low(e + 2)
                if e + 1 < NE + 1:
                    down_low(e + 1)

        @block.tensor
        def _(pe):
            def mm(out_, l, r, start=True, stop=True):
                return nc.tensor.matmul(out_, l, r, start=start, stop=stop)


            def fold_bias():
                pe.wait_ge(setup_in, SETUP)
                for half in range(2):
                    part = slice(half * D, (half + 1) * D)
                    for c in range(2):
                        last = mm(ps[6 + half][0:1, part], lnx_b[:, c:c + 1], wkv_raw[:, c, part], c == 0, c == 1)
                    last.then_inc(wkv_bias, 1)
                    if half == 0:
                        turn_context(0)

            def turn_latents():
                pe.wait_ge(ln_out, 2 * NT)
                for i in range(NT):
                    for c in range(2):
                        last = nc.tensor.transpose(ps[c][:, i * P:(i + 1) * P], big[:, i, c * P:(c + 1) * P], ident[:])
                last.then_inc(tok_T, 1)

            def latent_queries(i):
                pe.wait_ge(tok_T_evac, 2)
                pe.wait_ge(lat_in, LATENT)
                bank = ps[LATENT_BANK[i]]
                for c in range(2):
                    mm(bank[:, 0:D], xT[:, c, i * P:(i + 1) * P], wq[:, c, :], c == 0, c == 1)
                for c in range(2):
                    last = mm(bank[:, D:2 * D], xT[:, c, i * P:(i + 1) * P], wlkv[:, c, 0:D], c == 0, c == 1)
                last.then_inc(lat_mm, 1)

            def latent_values(k):
                if k >= 2:
                    pe.wait_ge(vlat_evac, k - 1)
                for b in (2 * k, 2 * k + 1):
                    for c in range(2):
                        last = mm(ps[k % 2][0:T, (b % 2) * D:(b % 2 + 1) * D], xT[:, c, b * T:(b + 1) * T], wlkv[:, c, D:2 * D], c == 0, c == 1)
                last.then_inc(vlat_mm, 1)

            def turn_queries():
                pe.wait_ge(lat_n, 2)
                for j in range(2):
                    for pair in range(NPAIR):
                        for i in range(NT):
                            last = nc.tensor.transpose(ps[LATENT_BANK[2 * j + pair]][:, i * P:(i + 1) * P], qk[:, j, i, pair * P:(pair + 1) * P], ident[:])
                        last.then_inc(lat_nT, 1)

            turned, keys_turned = [0], [0]

            def turn_context(n):
                b, g = divmod(n, NG)
                pe.wait_ge(xh_ready, n + 1)
                if n:
                    pe.wait_ge(xhT_low, n)
                if keys_turned[0]:
                    pe.wait_ge(kT_evac, keys_turned[0])
                turned[0] = n + 1
                for i, t in enumerate(tiles(g)):
                    for c in range(2):
                        last = nc.tensor.transpose(tx_bank[0:W, c * 256 + i * P:c * 256 + i * P + rows(t)],
                                                   xh[b % NXH][0:rows(t), t, c * HALF:c * HALF + W], ident[0:rows(t), 0:rows(t)])
                last.then_inc(xhT_mm, 1)

            def keys(n):
                g = n % NG
                pe.wait_ge(xhT_low, n + 1)
                if n >= 1:
                    pe.wait_ge(k_evac, n)
                for i, t in enumerate(tiles(g)):
                    for s, (x_, w_) in enumerate(((xhT, wkh), (xhTl, wkh), (xhT, wkl))):
                        for c in range(2):
                            k = HALF + c
                            last = mm(k_bank[0:rows(t), i * D:(i + 1) * D], x_[n % 2][0:k, c, i * P:i * P + rows(t)], w_[0:k, c, :],
                                      s == 0 and c == 0, s == 2 and c == 1)
                last.then_inc(k_mm, 1)

            def turn_keys(n):
                g = n % NG
                pe.wait_ge(k_n, n + 1)
                pe.wait_ge(xhT_low, turned[0])
                if n:
                    pe.wait_ge(kT_evac, n)
                for i, t in enumerate(tiles(g)):
                    for pair in range(NPAIR):
                        last = nc.tensor.transpose(tx_bank[:, pair * 256 + i * P:pair * 256 + i * P + rows(t)],
                                                   kn[n % 2][0:rows(t), i * D + pair * P:i * D + (pair + 1) * P], ident[0:rows(t), 0:rows(t)])
                last.then_inc(kT_mm, 1)
                keys_turned[0] = n + 1

            def scores(m):
                b, k = divmod(m, STEPS)
                pair, c = divmod(k, NCH)
                lo, hi = span(c)
                if m >= NCH:
                    pe.wait_ge(chunk_max, m - NCH + 1)
                pe.wait_ge(kT_evac, b * NG + min(2 * c + 2, NG))
                bank = score_bank[c][:, 0:hi - lo]
                q = qb[:, b * NPAIR + pair, :]
                if hi <= S:
                    last = mm(bank, q, kT[b % 2][:, pair, lo:hi])
                else:
                    mm(bank[:, 0:S - lo], q, kT[b % 2][:, pair, lo:S])
                    last = mm(bank[:, S - lo:hi - lo], q, klT[:, pair, b * T:(b + 1) * T])
                last.then_inc(score_mm, 1)

            def turn_probs(m):
                c = m % NCH
                j = m // NCH
                pe.wait_ge(exp_done, m + 1)
                if m >= 1:
                    pe.wait_ge(pT_evac, m)
                for i, (t, lo, hi) in enumerate(key_tiles(c)):
                    last = nc.tensor.transpose(tp_bank[0:hi - lo, i * P:(i + 1) * P], pr[j % 2][:, lo:hi], ident[:])
                if c == NCH - 1:
                    pe.wait_ge(plat_ready, j + 1)
                    last = nc.tensor.transpose(tp_bank[0:T, P:2 * P], plat[:], ident[:])
                last.then_inc(pT_mm, 1)

            def context_sum(m):
                b = m // STEPS
                c = m % NCH
                j = m // NCH
                pe.wait_ge(pT_evac, m + 1)
                if c == 0 and j >= 1:
                    pe.wait_ge(y_evac, j)
                for i, (t, lo, hi) in enumerate(key_tiles(c)):
                    last = mm(y_bank[:, 0:DC + 1], pT[m % 2][0:hi - lo, i, :], xh[b % NXH][0:hi - lo, t, 0:DC + 1], t == 0, t == FULL)
                if c == NCH - 1:
                    last.then_inc(y_mm, 1)

            def turn_sum(j):
                pe.wait_ge(y_evac, j + 1)
                pe.wait_ge(pT_evac, NCH * (j + 1) + (1 if NCH * (j + 1) < chunks else 0))
                nc.tensor.transpose(tp_bank[0:HALF, 0:P], ysb[:, 0:HALF], ident[:])
                nc.tensor.transpose(tp_bank[0:W, P:2 * P], ysb[:, HALF:DC + 1], ident[:]).then_inc(yT_mm, 1)

            def head_out(j):
                b, pair = divmod(j, NPAIR)
                pe.wait_ge(yT_evac, 2 * (j + 1))
                if NCH * (j + 1) + 1 < chunks:
                    pe.wait_ge(pT_evac, NCH * (j + 1) + 2)
                bank = tp_bank[:, 0:P]
                cols = slice(D + pair * P, D + (pair + 1) * P)
                mm(bank, wkv[0:HALF, 0, cols], yT[0:HALF, 0, :], True, False)
                mm(bank, wkv[0:W, 1, cols], yT[0:W, 1, :], False, False)
                mm(bank, vlat[:, b, pair * P:(pair + 1) * P], plT[:], False, True).then_inc(o_mm, 1)

            def project(i):
                pe.wait_ge(o_evac, 4 * NPAIR * (i + 1))
                if i == 0:
                    pe.wait_ge(mixer_in, MIXER)
                    pe.wait_ge(k_evac, groups)
                if i == 2:
                    pe.wait_ge(res_add, 1)
                bank = k_bank[:, (i % 2) * D:(i % 2 + 1) * D]
                for c in range(NPAIR):
                    mm(bank, oT[:, c, i * P:(i + 1) * P], wo[:, c, :], c == 0, False)
                last = mm(bank, ones_row[:], bo[:], False, True)
                if i % 2:
                    last.then_inc(res_mm, 1)

            def turn_tokens(k, bank):
                pe.wait_ge(ln_out, normed(2 + k))
                for i in (2 * (k % 2), 2 * (k % 2) + 1):
                    for c in range(2):
                        last = nc.tensor.transpose(bank[:, c * 2 * P + (i % 2) * P:c * 2 * P + (i % 2 + 1) * P], big[:, i, c * P:(c + 1) * P], ident[:])
                last.then_inc(tok_T, 1)

            def first_rates(half):
                part = slice(half * 2 * P, (half + 1) * 2 * P)
                pe.wait_ge(xx_ready, 2 * (half + 1))
                for c in range(2):
                    mm(ps[2 * half][:, 0:2 * P], wx0[:, c, 0:P], mixed[0][:, c, part], c == 0, c == 1)
                for c in range(2):
                    last = mm(ps[2 * half + 1][0:32, 0:2 * P], wx0[:, c, P:160], mixed[0][:, c, part], c == 0, c == 1)
                last.then_inc(xp_mm, 1)

            fold_bias()
            pe.wait_ge(wk_split, 3)
            for u in range(steps):
                n, m = group_of(u), chunk_of(u)
                prev = group_of(u - 2) if u >= 2 else None
                if prev is not None:
                    turn_keys(prev)
                if n is not None:
                    keys(n)
                m6, m7 = lag(u, 6), lag(u, 7)
                if m6 is not None and m6 % NCH == NCH - 1:
                    turn_sum(m6 // NCH)
                if m7 is not None and m7 % NCH == NCH - 1:
                    head_out(m7 // NCH)
                if n is not None and n + 1 < groups:
                    turn_context(n + 1)
                if m == 0:
                    pe.wait_ge(lat_nT_evac, 1)
                    pe.wait_ge(lat_kT_evac, 1)
                    pe.wait_ge(vlat_evac, 4)
                if m is not None:
                    scores(m)
                if m6 is not None and m6 % NCH == NCH - 1:
                    pe.wait_ge(yT_evac, 2 * (m6 // NCH + 1))
                if m7 is not None and m7 % NCH == NCH - 1:
                    pe.wait_ge(o_evac, 2 * (m7 // NCH + 1))
                if lag(u, 4) is not None:
                    turn_probs(lag(u, 4))
                if lag(u, 5) is not None:
                    context_sum(lag(u, 5))
                if u == 3:
                    turn_latents()
                if u in (4, 5):
                    latent_queries(2 * (u - 4))
                    latent_queries(2 * (u - 4) + 1)
                if u in (6, 7):
                    latent_values(2 * (u - 6))
                    latent_values(2 * (u - 6) + 1)
                if u == 7:
                    turn_queries()
                if u == B * STEPS + 2:
                    project(0)
                    project(1)
                if u == B * STEPS + 5:
                    turn_tokens(0, tx_bank)
                if u == B * STEPS + 10:
                    project(2)
                    first_rates(0)

            project(3)
            turn_tokens(1, tx_bank)
            first_rates(1)
            pe.wait_ge(xp_act, 4)
            def rates(k):
                i = ORDER[k]
                for c in range(2):
                    s = 2 * k + c
                    if s >= 4:
                        pe.wait_ge(mu_use, s - 3)
                    if i < 4:
                        mm(ps[s % 4][:], wx2a[:, i, c * P:(c + 1) * P], xpa[:]).then_inc(mu_mm, 1)
                    else:
                        mm(ps[s % 4][:], wx2b[:, c * P:(c + 1) * P], xpb[:]).then_inc(mu_mm, 1)

            def wait_mixed(k):
                pe.wait_ge(mixed_even, k + 1)
                pe.wait_ge(mixed_odd, k + 1)

            pe.wait_ge(wx2_in, 4 * 16)
            rates(0)
            rates(1)
            wait_mixed(0)
            for c in range(2):
                last = mm(ps[5][0:64, :], ww1[:, c, :], mixed[1][:, c, :], c == 0, c == 1)
            last.then_inc(w1_mm, 1)
            rates(2)
            wait_mixed(1)
            for c in range(2):
                last = mm(ps[4][:], wr[:, c, :], mixed[0][:, c, :], c == 0, c == 1)
            last.then_inc(r_mm, 1)
            rates(3)
            pe.wait_ge(w1_act, 1)
            for i in range(NT):
                last = mm(ps[7][:, i * P:(i + 1) * P], wt[:, i * P:(i + 1) * P], ww2[:])
            last.then_inc(w2_mm, 1)
            wait_mixed(2)
            for c in range(2):
                last = mm(ps[6][:], wk[:, c, :], mixed[2][:, c, :], c == 0, c == 1)
            last.then_inc(kk_mm, 1)
            rates(4)
            pe.wait_ge(w2_act, 1)
            pe.wait_ge(r_evac, 1)
            pe.wait_ge(kk_evac, 1)
            for half in range(2):
                for i in range(NT):
                    s = NT * half + i
                    if s >= 4:
                        pe.wait_ge(e_act, s - 3)
                    mm(ps[4 + s % 4][:, 0:3 * P], ew[:, i, :], sums[:, 3 * half:3 * half + 3, :].rearrange("p l n -> p (l n)")).then_inc(e_mm, 1)
            pe.wait_ge(mu_use, 10)
            pe.wait_ge(ruk_ready, 1)
            for i in range(NT):
                last = mm(ps[3][:, 4 * i:4 * i + 4], ruk[:, i * P:(i + 1) * P], headsel[:])
            last.then_inc(dc_mm, 1)

            def values(k):
                wait_mixed(3)
                for i in (2 * k, 2 * k + 1):
                    for c in range(2):
                        last = mm(ps[k][:, (i % 2) * D:(i % 2 + 1) * D], mixed[3][:, c, i * P:(i + 1) * P], wv[:, c, :], c == 0, c == 1)
                last.then_inc(v_mm, 1)

            def gates(k):
                wait_mixed(4)
                if k == 1:
                    pe.wait_ge(vec, 1)
                for i in (2 * k, 2 * k + 1):
                    for c in range(2):
                        last = mm(ps[2 + k][:, (i % 2) * D:(i % 2 + 1) * D], mixed[4][:, c, i * P:(i + 1) * P], wg[:, c, :], c == 0, c == 1)
                last.then_inc(g_mm, 1)

            def weights(lv):
                if lv == 0:
                    pe.wait_ge(e_act, 2 * NT)
                if lv >= 2:
                    pe.wait_ge(a_pick, lv - 1)
                pe.wait_ge(left_ready, lv + 1)
                pe.wait_ge(right_ready, lv + 1)
                for i in range(NT):
                    last = mm(ps[4 + 2 * (lv % 2) + i // 2][:, (i % 2) * 2 * P:(i % 2 + 1) * 2 * P], ex[:, lv, i * P:(i + 1) * P],
                              rblk[lv % 2][:, i].rearrange("p h q -> p (h q)"))
                last.then_inc(a_mm, 1)

            def weigh(half):
                pe.wait_ge(a_pick, LEVELS)
                pe.wait_ge(v_centred, 1)
                for i in (2 * half, 2 * half + 1):
                    for h in range(H):
                        last = mm(ps[4 + half][:, (i % 2) * D + h * DH:(i % 2) * D + (h + 1) * DH], aT[:, i, h, :], vn[:, i, h * DH:(h + 1) * DH])
                last.then_inc(av_mm, 1)

            def turn_gated(half):
                pe.wait_ge(o_gated, half + 1)
                for i in (2 * half, 2 * half + 1):
                    for c in range(2):
                        last = nc.tensor.transpose(ps[6 + half][:, c * 2 * P + (i % 2) * P:c * 2 * P + (i % 2 + 1) * P], on[:, i, c * P:(c + 1) * P], ident[:])
                last.then_inc(oT2_mm, 1)

            def project_mixer(half):
                pe.wait_ge(oT2_evac, half + 1)
                pe.wait_ge(g_act, 2)
                for i in (2 * half, 2 * half + 1):
                    for c in range(2):
                        last = mm(ps[2 + half][:, (i % 2) * D:(i % 2 + 1) * D], oT2[:, c, i * P:(i + 1) * P], wo2[:, c, :], c == 0, c == 1)
                last.then_inc(res_mm, 1)

            values(0)
            for lv in range(LEVELS):
                weights(lv)
                if lv == 0:
                    values(1)
                if lv in (1, 2):
                    gates(lv - 1)
            weigh(0)
            weigh(1)
            for half in range(2):
                turn_gated(half)
                project_mixer(half)
            pe.wait_ge(v_evac, 2)
            turn_tokens(2, ps[0])
            def router(half):
                pe.wait_ge(tok_T_evac, 5 + half)
                for i in (2 * half, 2 * half + 1):
                    for c in range(2):
                        last = mm(ps[6][:, i * NE:(i + 1) * NE], xT[:, c, i * P:(i + 1) * P], gatew[:, c, :], c == 0, c == 1)
                last.then_inc(gate_mm, 1)

            pe.wait_ge(oT2_evac, 2)
            router(0)
            turn_tokens(3, ps[1])
            router(1)
            pe.wait_ge(x_low, 2)
            pe.wait_ge(res_add, 4)
            PASSES = ((0, 0), (1, 0), (0, 1))

            def down(e):
                pe.wait_ge(inter_low, e + 1)
                pe.wait_ge(ed_low, e + 1)
                for i in range(NT):
                    if e >= 2 and i % 2 == 0:
                        pe.wait_ge(acc_done, (e - 2) * NT + i + 2)
                    for s, (x_, w_) in enumerate(PASSES):
                        last = mm(ps[4 + 2 * (e % 2) + i // 2][:, (i % 2) * D:(i % 2 + 1) * D], inter_part[x_][:, i * P:(i + 1) * P], down_part[e % 2][w_], s == 0, s == 2)
                    if i % 2:
                        last.then_inc(down_mm, 1)

            for e in range(NE + 1):
                if e >= 2:
                    pe.wait_ge(inter_ready, e - 1)
                pe.wait_ge(gu_low, e + 1)
                for j in range(2):
                    for s, (x_, w_) in enumerate(PASSES):
                        for c in range(2):
                            last = mm(ps[2 * (e % 2) + j][:], gu_part[e % 2][w_][:, j, c * INTER:(c + 1) * INTER], x_part[x_][:, c, :], s == 0 and c == 0, s == 2 and c == 1)
                    last.then_inc(gu_mm, 1)
                if e >= 1:
                    down(e - 1)
            down(NE)

        @block.scalar
        def _(act):
            A = nc.scalar.activation
            def evac_latents():
                act.wait_ge(setup_in, SETUP)
                act.wait_ge(tok_T, 1)
                for c in range(2):
                    A(xT[:, c, :], ps[c][:], ACT.Identity, bias=lnl_b[:, c:c + 1], scale=lnl_g[:, c:c + 1]).then_inc(tok_T_evac, 1)

            def square_latents(i):
                act.wait_ge(lat_mm, i + 1)
                A(kn_sq(i), ps[LATENT_BANK[i]][:], ACT.Square).then_inc(lat_sq, 1)

            def evac_values(k):
                act.wait_ge(vlat_mm, k + 1)
                A(vlat[:, 2 * k:2 * k + 2, :], ps[k % 2][0:T, :], ACT.Copy).then_inc(vlat_evac, 1)

            def evac_queries():
                for pair in range(NPAIR):
                    act.wait_ge(lat_nT, pair + 1)
                    for h in range(2):
                        part = slice(h * DH, (h + 1) * DH)
                        last = A(qb[part, pair::NPAIR, h * T:(h + 1) * T], ps[2 + pair][part, :].rearrange("p (b t) -> p b t", b=B), ACT.Copy,
                                 scale=qkg[part, 0:1])
                last.then_inc(lat_nT_evac, 1)

            def evac_context(n):
                act.wait_ge(xhT_mm, n + 1)
                k = 256 if n % NG < NG - 1 else TAIL
                A(xhT[n % 2][:, :, 0:k], tx_bank[0:W, :].rearrange("p (c k) -> p c k", c=2)[:, :, 0:k], ACT.Copy).then_inc(xhT_evac, 1)

            def square_keys(n):
                act.wait_ge(k_mm, n + 1)
                if n >= 1:
                    act.wait_ge(k_ss, n)
                r, k = rows(tiles(n % NG)[0]), D * len(tiles(n % NG))
                A(ksq[0:r, 0:k], k_bank[0:r, 0:k], ACT.Square).then_inc(k_sq, 1)

            def copy_keys(n):
                if n >= 2:
                    act.wait_ge(k_n, n - 1)
                r, k = rows(tiles(n % NG)[0]), D * len(tiles(n % NG))
                A(kraw[n % 2][0:r, 0:k], k_bank[0:r, 0:k], ACT.Copy).then_inc(k_evac, 1)

            def evac_keys(n):
                b, g = divmod(n, NG)
                act.wait_ge(kT_mm, n + 1)
                k = 256 if g < NG - 1 else TAIL
                A(kT[b % 2][:, :, 256 * g:256 * g + k], tx_bank[:].rearrange("p (c k) -> p c k", c=2)[:, :, 0:k], ACT.Copy).then_inc(kT_evac, 1)

            def exponentials(m):
                j, c = divmod(m, NCH)
                act.wait_ge(row_max, j + 1)
                lo, hi = span(c)
                A(pr[j % 2][:, lo:hi], pr[j % 2][:, lo:hi], ACT.Exp, bias=nm[:, j % 2:j % 2 + 1], accum_out=ls[:, j % 2, c:c + 1]).then_inc(exp_done, 1)

            def evac_probs(m):
                c = m % NCH
                act.wait_ge(pT_mm, m + 1)
                if c < NCH - 1:
                    A(pT[m % 2].rearrange("p i q -> p (i q)"), tp_bank[:], ACT.Copy).then_inc(pT_evac, 1)
                else:
                    A(plT[:], tp_bank[0:T, P:2 * P], ACT.Copy)
                    A(pT[m % 2][0:TAIL, 0, :], tp_bank[0:TAIL, 0:P], ACT.Copy).then_inc(pT_evac, 1)

            def evac_tokens(k, bank):
                act.wait_ge(tok_T, 2 + k)
                A(xT[:, :, (k % 2) * 2 * P:(k % 2 + 1) * 2 * P], bank[:].rearrange("p (c k) -> p c k", c=2), ACT.Copy).then_inc(tok_T_evac, 1)

            def first_tanh(half):
                part = slice(half * 2 * P, (half + 1) * 2 * P)
                act.wait_ge(xp_mm, half + 1)
                A(xpa[:, part], ps[2 * half][:, 0:2 * P], ACT.Tanh).then_inc(xp_act, 1)
                A(xpb[:, part], ps[2 * half + 1][0:32, 0:2 * P], ACT.Tanh).then_inc(xp_act, 1)

            evac_context(0)
            for u in range(steps):
                n = group_of(u)
                prev = group_of(u - 2) if u >= 2 else None
                if prev is not None:
                    evac_keys(prev)
                m4 = lag(u, 4)
                if m4 is not None and m4 % NCH < NCH - 1:
                    exponentials(m4)
                    if m4 % NCH == NCH - 2:
                        exponentials(m4 + 1)
                m6, m7 = lag(u, 6), lag(u, 7)
                if m6 is not None and m6 % NCH == NCH - 1:
                    j = m6 // NCH
                    act.wait_ge(yT_mm, j + 1)
                    A(yT[0:HALF, 0, :], tp_bank[0:HALF, 0:P], ACT.Copy).then_inc(yT_evac, 1)
                    A(yT[:, 1, :], tp_bank[0:W, P:2 * P], ACT.Copy).then_inc(yT_evac, 1)
                if m7 is not None and m7 % NCH == NCH - 1:
                    j = m7 // NCH
                    b, pair = divmod(j, NPAIR)
                    act.wait_ge(o_mm, j + 1)
                    for h in range(2):
                        part = slice(h * DH, (h + 1) * DH)
                        A(oT[part, pair, b * T:(b + 1) * T], tp_bank[part, h * T:(h + 1) * T], ACT.Copy).then_inc(o_evac, 1)
                if n is not None:
                    square_keys(n)
                    if n + 1 < groups:
                        evac_context(n + 1)
                    copy_keys(n)
                if m4 is not None:
                    evac_probs(m4)
                if u == 3:
                    evac_latents()
                if u in (4, 5):
                    square_latents(2 * (u - 4))
                    square_latents(2 * (u - 4) + 1)
                if u in (6, 7):
                    evac_values(2 * (u - 6))
                    evac_values(2 * (u - 6) + 1)
                if u == 7:
                    evac_queries()
                if u == B * STEPS + 5:
                    evac_tokens(0, tx_bank)

            act.wait_ge(mixer_in, MIXER)
            first_tanh(0)
            evac_tokens(1, tx_bank)
            first_tanh(1)
            act.wait_ge(w1_mm, 1)
            A(wt[0:64, :], ps[5][0:64, :], ACT.Tanh).then_inc(w1_act, 1)
            act.wait_ge(r_mm, 1)
            A(rT[:], ps[4][:], ACT.Copy).then_inc(r_evac, 1)
            act.wait_ge(w2_mm, 1)
            A(ew[:], ps[7][:], ACT.Exp).then_inc(w2_act, 1)
            act.wait_ge(kk_mm, 1)
            A(rkT[:], ps[6][:], ACT.Copy).then_inc(kk_evac, 1)
            for s in range(2 * NT):
                half, i = divmod(s, NT)
                act.wait_ge(e_mm, s + 1)
                A(ex[:, 3 * half:3 * half + 3, i * P:(i + 1) * P], ps[4 + s % 4][:, 0:3 * P].rearrange("p (l n) -> p l n", l=3), ACT.Exp, scale=-1.0).then_inc(e_act, 1)
            for j in range(2):
                act.wait_ge(v_mm, j + 1)
                A(vn[:, 2 * j:2 * j + 2, :], ps[j][:], ACT.Copy).then_inc(v_evac, 1)
            for j in range(2):
                act.wait_ge(g_mm, j + 1)
                A(sg[:, 2 * j:2 * j + 2, :], ps[2 + j][:], ACT.Silu).then_inc(g_act, 1)

            def gate_up_high(e):
                if e >= 2:
                    act.wait_ge(gu_mm, 2 * (e - 1))
                A(gu_part[e % 2][0].rearrange("p a b -> p (a b)"), experts[:, e, 0:512], ACT.Copy).then_inc(gu_high, 1)

            def down_high(e):
                if e >= 2:
                    act.wait_ge(down_mm, 2 * (e - 1))
                A(down_part[e % 2][0], ed[:, e, :], ACT.Copy).then_inc(ed_high, 1)

            act.wait_ge(expert_in, EXPERT)
            gate_up_high(0)
            gate_up_high(1)
            down_high(0)
            for half in range(2):
                tl = slice(2 * half, 2 * half + 2)
                act.wait_ge(av_mm, half + 1)
                A(big[:, tl, :], ps[4 + half][:].rearrange("p (i d) -> p i d", i=2), ACT.Square).then_inc(o_sq, 1)
            for half in range(2):
                act.wait_ge(oT2_mm, half + 1)
                A(oT2[:, :, half * 2 * P:(half + 1) * 2 * P], ps[6 + half][:].rearrange("p (c k) -> p c k", c=2), ACT.Copy).then_inc(oT2_evac, 1)
            for half in range(2):
                evac_tokens(2 + half, ps[half])
                part = slice(half * 2 * P, (half + 1) * 2 * P)
                A(x_part[0][:, :, part], ps[half][:].rearrange("p (c k) -> p c k", c=2), ACT.Copy).then_inc(x_high, 1)
            act.wait_ge(gate_mm, 2)
            A(fe[:, 0], ps[6][:, 0:NT * NE], ACT.Exp, scale=-1.0).then_inc(gate_exp, 1)
            for e in range(NE + 1):
                act.wait_ge(gu_mm, 2 * e + 1)
                if e >= 2:
                    act.wait_ge(inter_ready, e - 1)
                A(sil[e % 2][:], ps[2 * (e % 2)][:], ACT.Silu).then_inc(silu, 1)
                if e + 2 < NE + 1:
                    gate_up_high(e + 2)
                act.wait_ge(inter_ready, e + 1)
                if e >= 1:
                    act.wait_ge(down_mm, 2 * e)
                A(inter_part[0], inter[e % 2][:], ACT.Copy).then_inc(inter_high, 1)
                if e + 1 < NE + 1:
                    down_high(e + 1)

        @block.vector
        def _(dve):
            V = nc.vector
            tick = [0]

            def then(ins):
                tick[0] += 1
                ins.then_inc(vec_tick, 1)
                dve.wait_ge(vec_tick, tick[0])

            def norm_stats(n, src):
                lo, hi = NORMS[n]
                for i in range(lo, hi):
                    V.bn_stats(st[:, i, :], src[:, i, :]).then_inc(ln_stats, 1)
                dve.wait_ge(ln_stats, normed(n))
                for i in range(lo, hi):
                    last = V.bn_aggr(mv[:, i, :], st[:, i, :])
                last.then_inc(ln_aggr, 1)

            def norm_apply(n, src, dst):
                dve.wait_ge(ln_rstd, n + 1)
                for i in range(*NORMS[n]):
                    V.tensor_scalar(dst[:, i, :], src[:, i, :], mv[:, i, 0:1], rs[:, i:i + 1], ALU.subtract, ALU.mult).then_inc(ln_out, 1)

            def norm_tokens(n, src, dst):
                norm_stats(n, src)
                norm_apply(n, src, dst)

            def group_stats(n):
                b, g = divmod(n, NG)
                if n == 0:
                    dve.wait_ge(ctx_first, 16)
                if g == (0 if b else 2):
                    dve.wait_ge(ctx_in[b % 2], 32 * (b // 2 + 1))
                for i, t in enumerate(tiles(g)):
                    last = V.bn_stats(cst[0:rows(t), n % 2, i, :], xh[b % NXH][0:rows(t), t, 0:DC])
                last.then_inc(cstat, 1)
                dve.wait_ge(cstat, n + 1)
                for i, t in enumerate(tiles(g)):
                    last = V.bn_aggr(cmv[0:rows(t), n % 2, i, :], cst[0:rows(t), n % 2, i, :])
                last.then_inc(caggr, 1)

            def normalise(n):
                b, g = divmod(n, NG)
                dve.wait_ge(crstd, n + 1)
                for i, t in enumerate(tiles(g)):
                    r = rows(t)
                    last = V.tensor_scalar(xh[b % NXH][0:r, t, 0:DC], xh[b % NXH][0:r, t, 0:DC], cmv[0:r, n % 2, i, 0:1], crs[0:r, n % 2, i:i + 1], ALU.subtract, ALU.mult)
                last.then_inc(xh_ready, 1)

            dve.wait_ge(pool_const, 1)
            group_stats(0)
            group_stats(1)
            dve.wait_ge(setup_in, SETUP)
            for c in range(2):
                V.tensor_scalar(wkv[0:HALF, c, :], wkv_raw[:, c, :], lnx_g[:, c:c + 1], None, ALU.mult)
            V.scalar_tensor_tensor(qkg[:], qg[:], DH ** -0.5, kg[:], ALU.mult, ALU.mult)
            normalise(0)
            normalise(1)
            dve.wait_ge(wkv_bias, 1)
            V.tensor_copy(wkv[HALF:W, 1, 0:D], ps[6][0:1, 0:D]).then_inc(wkv_ready, 1)
            dve.wait_ge(wkv_ready, 1)
            parts = ((slice(0, HALF), 0), (slice(0, W), 1))
            for p_, c in parts:
                V.tensor_copy(wkh[p_, c, :], wkv[p_, c, 0:D]).then_inc(wk_split, 1)
            dve.wait_ge(wk_split, 2)
            for p_, c in parts:
                last = V.tensor_tensor(wkl[p_, c, :], wkv[p_, c, 0:D], wkh[p_, c, :].bitcast(F32), ALU.subtract)
            last.then_inc(wk_split, 1)
            dve.wait_ge(wkv_bias, 2)
            V.tensor_copy(wkv[HALF:W, 1, D:2 * D], ps[7][0:1, D:2 * D]).then_inc(wkv_ready, 1)

            def latent_sums(i):
                dve.wait_ge(lat_sq, i + 1)
                sq = kn_sq(i).rearrange("p (j h d) -> p j h d", j=2, h=H)
                for j in range(2):
                    V.tensor_reduce(qkss[:, (j * NT + i) * H:(j * NT + i + 1) * H], sq[:, j], AX.X, ALU.add).then_inc(lat_ss, 1)

            def scale_latents(half):
                dve.wait_ge(lat_r, half + 1)
                for i in (2 * half, 2 * half + 1):
                    for j in range(2):
                        last = V.tensor_tensor(qk[:, j, i, :].rearrange("p (h d) -> p h d", h=H),
                                               ps[LATENT_BANK[i]][:, j * D:(j + 1) * D].rearrange("p (h d) -> p h d", h=H),
                                               qkr[:, (j * NT + i) * H:(j * NT + i + 1) * H].unsqueeze(2).broadcast_to([P, H, DH]), ALU.mult)
                last.then_inc(lat_n, 1)

            def evac_latent_keys():
                for pair in range(NPAIR):
                    dve.wait_ge(lat_nT, 3 + pair)
                    last = V.tensor_copy(klT[:, pair, :], ps[6 + pair][:])
                last.then_inc(lat_kT_evac, 1)

            def key_sums(n):
                dve.wait_ge(k_sq, n + 1)
                r, k = rows(tiles(n % NG)[0]), len(tiles(n % NG))
                V.tensor_reduce(kss[0:r, n % 2, 0:4 * k], ksq[0:r, 0:D * k].rearrange("p (h d) -> p h d", d=DH), AX.X, ALU.add).then_inc(k_ss, 1)

            def scale_keys(n):
                dve.wait_ge(k_r, n + 1)
                dve.wait_ge(k_evac, n + 1)
                if n >= 2:
                    dve.wait_ge(kT_mm, n - 1)
                r, k = rows(tiles(n % NG)[0]), len(tiles(n % NG))
                V.tensor_tensor(kn[n % 2][0:r, 0:D * k].rearrange("p (h d) -> p h d", d=DH), kraw[n % 2][0:r, 0:D * k].rearrange("p (h d) -> p h d", d=DH),
                                kr[0:r, n % 2, 0:4 * k].unsqueeze(2).broadcast_to([r, 4 * k, DH]), ALU.mult).then_inc(k_n, 1)

            def split_context(n):
                dve.wait_ge(xhT_evac, n + 1)
                k = 256 if n % NG < NG - 1 else TAIL
                turned = tx_bank[0:W, :].rearrange("p (c k) -> p c k", c=2)[:, :, 0:k]
                V.tensor_tensor(xhTl[n % 2][:, :, 0:k], turned, xhT[n % 2][:, :, 0:k].bitcast(F32), ALU.subtract).then_inc(xhT_low, 1)

            def maxima(m):
                j, c = divmod(m, NCH)
                lo, hi = span(c)
                dve.wait_ge(score_mm, m + 1)
                if j % NPAIR == 0 and c == 0:
                    dve.wait_ge(mask_spread, j // NPAIR + 1)
                V.tensor_tensor_reduce(pr[j % 2][:, lo:hi], score_bank[c][:, 0:hi - lo], mask_bc[(j // NPAIR) % 2][:, lo:hi], 1.0, LOWEST,
                                       ALU.add, ALU.max, mx[:, j % 2, c:c + 1]).then_inc(chunk_max, 1)
                if c == NCH - 1:
                    dve.wait_ge(chunk_max, m + 1)
                    V.tensor_reduce(nm[:, j % 2:j % 2 + 1], mx[:, j % 2, :], AX.X, ALU.max, negate=True).then_inc(row_max, 1)

            def latent_probs(j):
                dve.wait_ge(exp_done, NCH * (j + 1))
                V.tensor_reduce(lsum[:, j % 2:j % 2 + 1], ls[:, j % 2, :], AX.X, ALU.add).then_inc(row_sum, 1)
                dve.wait_ge(row_sum, j + 1)
                V.reciprocal(rl[:, j % 2:j % 2 + 1], lsum[:, j % 2:j % 2 + 1]).then_inc(row_inv, 1)
                dve.wait_ge(row_inv, j + 1)
                V.tensor_scalar(plat[:], pr[j % 2][:, S:KEYS], rl[:, j % 2:j % 2 + 1], None, ALU.mult).then_inc(plat_ready, 1)

            def evac_sum(j):
                dve.wait_ge(y_mm, j + 1)
                V.tensor_scalar(ysb[:, 0:DC + 1], y_bank[:, 0:DC + 1], rl[:, j % 2:j % 2 + 1], None, ALU.mult).then_inc(y_evac, 1)

            def residual_stats(half):
                tl = slice(2 * half, 2 * half + 2)
                dve.wait_ge(res_mm, half + 1)
                V.tensor_tensor(X[:, tl, :], X[:, tl, :], k_bank[:].rearrange("p (i d) -> p i d", i=2), ALU.add).then_inc(res_add, 1)
                dve.wait_ge(res_add, half + 1)
                norm_stats(2 + half, X)

            def differences(half):
                dve.wait_ge(tok_T_evac, 3 + half)
                part = slice(half * 2 * P, (half + 1) * 2 * P)
                for c in range(2):
                    xv = xT[:, c, part].rearrange("p (b t) -> p b t", t=T)
                    dv = delta[:, c, part].rearrange("p (b t) -> p b t", t=T)
                    V.tensor_tensor(dv[:, :, 1:T], xv[:, :, 0:T - 1], xv[:, :, 1:T], ALU.subtract)
                    V.tensor_scalar(dv[:, :, 0:1], xv[:, :, 0:1], -1.0, None, ALU.mult).then_inc(d_ready, 1)
                for c in range(2):
                    dve.wait_ge(d_ready, 2 * half + c + 1)
                    V.scalar_tensor_tensor(mixed[0][:, c, part], delta[:, c, part], mu0[:, c:c + 1], xT[:, c, part], ALU.mult, ALU.add).then_inc(xx_ready, 1)

            split_context(0)
            for u in range(steps):
                n, m = group_of(u), chunk_of(u)
                m4, m5 = lag(u, 4), lag(u, 5)
                prev = group_of(u - 1) if u else None
                if m4 is not None and m4 % NCH == NCH - 1:
                    latent_probs(m4 // NCH)
                if n is not None and n + 2 < groups:
                    group_stats(n + 2)
                if prev is not None:
                    scale_keys(prev)
                if n is not None:
                    key_sums(n)
                    if n + 1 < groups:
                        split_context(n + 1)
                    if n + 2 < groups:
                        normalise(n + 2)
                if m is not None:
                    maxima(m)
                if m5 is not None and m5 % NCH == NCH - 1:
                    evac_sum(m5 // NCH)
                if u == 0:
                    dve.wait_ge(x_in, 16)
                    norm_stats(0, X)
                if u == 1:
                    norm_apply(0, X, xn)
                    dve.wait_ge(ln_out, NT)
                    norm_stats(1, xn)
                if u == 2:
                    norm_apply(1, xn, big)
                if u in (4, 5):
                    latent_sums(2 * (u - 4))
                    latent_sums(2 * (u - 4) + 1)
                if u in (6, 7):
                    scale_latents(u - 6)
                if u == 7:
                    evac_latent_keys()
                if u == B * STEPS + 3:
                    residual_stats(0)
                if u == B * STEPS + 4:
                    norm_apply(2, X, big)
                if u == B * STEPS + 9:
                    differences(0)

            residual_stats(1)
            norm_apply(3, X, big)
            differences(1)
            for k, i in enumerate(ORDER):
                for c in range(2):
                    s = 2 * k + c
                    dve.wait_ge(mu_mm, s + 1)
                    if c == 1 and k:
                        dve.wait_ge(mixed_odd, k)
                    V.scalar_tensor_tensor(tmix[c][:], ps[s % 4][:], xbias[:, c, i:i + 1], delta[:, c, :], ALU.add, ALU.mult).then_inc(mu_use, 1)
                    if c == 1:
                        dve.wait_ge(mu_use, s)
                        V.tensor_tensor(mixed[i][:, 0, :], tmix[0][:], xT[:, 0, :], ALU.add).then_inc(mixed_even, 1)
                        dve.wait_ge(mixed_even, k + 1)
            dve.wait_ge(r_evac, 1)
            dve.wait_ge(kk_evac, 1)
            V.scalar_tensor_tensor(ruk[:], rT[:], bonus[:, 0:1], rkT[:], ALU.mult, ALU.mult).then_inc(ruk_ready, 1)

            def right_side(lv):
                dve.wait_ge(e_act, NT * (lv // 3 + 1))
                dve.wait_ge(r_zero, lv % 2 + 1)
                if lv >= 2:
                    dve.wait_ge(a_mm, lv - 1)
                for h in range(H):
                    part = slice(32 * h, 32 * h + 32)
                    right = lambda v: v.rearrange("p (n s m) -> p n s m", s=2, m=1 << lv)[:, :, 1]
                    last = V.tensor_tensor(rblk[lv % 2][part, :, h, :].rearrange("p i (n m) -> p i n m", m=1 << lv),
                                           right(ex[part, lv, :]).rearrange("p (i n) m -> p i n m", i=NT),
                                           right(rT[part]).rearrange("p (i n) m -> p i n m", i=NT), ALU.mult)
                last.then_inc(right_ready, 1)

            def heads(t_, half):
                return t_[:, 2 * half:2 * half + 2, :].rearrange("p i (h d) -> p (i h) d", h=H)

            def pick_weights(lv):
                dve.wait_ge(a_mm, lv + 1)
                if lv:
                    dve.wait_ge(a_pick, lv)
                for k in range(2):
                    last = V.copy_predicated(aT[:, 2 * k:2 * k + 2].rearrange("p i h (n s m) -> p (i h) n s m", s=2, m=1 << lv)[:, :, :, 1, :],
                                             pick[:, lv, :].rearrange("p (n m) -> p n m", m=1 << lv).unsqueeze(1).broadcast_to([P, 2 * H, P // 2 >> lv, 1 << lv]),
                                             ps[4 + 2 * (lv % 2) + k][:].rearrange("p (x n m) -> p x n m", x=2 * H, m=1 << lv))
                last.then_inc(a_pick, 1)

            def variance(half):
                dve.wait_ge(o_sq, half + 1)
                V.tensor_reduce(hs[:, 1, 2 * H * half:2 * H * (half + 1)], heads(big, half), AX.X, ALU.add).then_inc(gn_var, 1)
                tl = slice(2 * half, 2 * half + 2)
                dve.wait_ge(gain_ready, half + 1)
                V.tensor_tensor(on[:, tl, :], ps[4 + half][:].rearrange("p (i d) -> p i d", i=2), sg[:, tl, :], ALU.mult).then_inc(o_gain, 1)

            def gate(half):
                part = slice(2 * H * half, 2 * H * (half + 1))
                tl = slice(2 * half, 2 * half + 2)
                dve.wait_ge(gn_r, half + 1)
                dve.wait_ge(o_gain, half + 1)
                then(V.tensor_tensor(heads(on, half), heads(on, half), hs[:, 2, part].unsqueeze(2).broadcast_to([P, 2 * H, DH]), ALU.mult))
                V.tensor_tensor(on[:, tl, :], on[:, tl, :], sgb[:, tl, :], ALU.add).then_inc(o_gated, 1)

            def residual_mixer(half):
                tl = slice(2 * half, 2 * half + 2)
                dve.wait_ge(res_mm, 3 + half)
                V.tensor_tensor(acc[:, tl, :], X[:, tl, :], ps[2 + half][:].rearrange("p (i d) -> p i d", i=2), ALU.add).then_inc(res_add, 1)
                dve.wait_ge(res_add, 3 + half)
                norm_tokens(4 + half, acc, big)

            right_side(0)
            right_side(1)
            dve.wait_ge(dc_mm, 1)
            V.tensor_copy(dcoef[:], ps[3][:, 0:4 * NT]).then_inc(vec, 1)
            dve.wait_ge(vec, 1)
            V.tensor_tensor(aT[:, 2:4].rearrange("p i h t -> p (i h) t"), ident[:].unsqueeze(1).broadcast_to([P, 2 * H, P]),
                            dcoef[:, 2:4, :].rearrange("p i h -> p (i h)").unsqueeze(2).broadcast_to([P, 2 * H, P]), ALU.mult).then_inc(a_last, 1)
            dve.wait_ge(a_last, 1)
            dve.wait_ge(a_first, 1)
            for lv in range(LEVELS):
                pick_weights(lv)
                if lv + 2 < LEVELS:
                    right_side(lv + 2)
                if lv == 0:
                    hv = vn.rearrange("p i (h d) -> p (i h) d", h=H)
                    dve.wait_ge(v_evac, 2)
                    then(V.tensor_reduce(hs[:, 0, :], hv, AX.X, ALU.add))
                    then(V.tensor_scalar(hs[:, 3, :], hs[:, 0, :], 1.0 / DH, None, ALU.mult))
                    V.tensor_tensor(hv, hv, hs[:, 3, :].unsqueeze(2).broadcast_to([P, NT * H, DH]), ALU.subtract).then_inc(v_centred, 1)
            variance(0)
            variance(1)
            gate(0)
            gate(1)
            residual_mixer(0)
            residual_mixer(1)

            for half in range(2):
                dve.wait_ge(x_high, half + 1)
                part = slice(half * 2 * P, (half + 1) * 2 * P)
                V.tensor_tensor(x_part[1][:, :, part], xT[:, :, part], x_part[0][:, :, part].bitcast(F32), ALU.subtract).then_inc(x_low, 1)
            def gated(e):
                dve.wait_ge(silu, e + 1)
                dve.wait_ge(gu_mm, 2 * e + 2)
                V.tensor_tensor(inter[e % 2][:], sil[e % 2][:], ps[2 * (e % 2) + 1][:], ALU.mult).then_inc(inter_ready, 1)

            def gated_low(e):
                dve.wait_ge(inter_high, e + 1)
                V.tensor_tensor(inter_part[1], inter[e % 2][:], inter_part[0].bitcast(F32), ALU.subtract).then_inc(inter_low, 1)

            def accumulate(e, tls):
                for i in tls:
                    dve.wait_ge(down_mm, 2 * e + i // 2 + 1)
                    if e >= 1:
                        dve.wait_ge(acc_done, NT * (e - 1) + i + 1)
                    y = ps[4 + 2 * (e % 2) + i // 2][:, (i % 2) * D:(i % 2 + 1) * D]
                    if e >= 1:
                        V.scalar_tensor_tensor(acc[:, i, :], y, fe[:, 7, i, e - 1:e], acc[:, i, :], ALU.mult, ALU.add).then_inc(acc_done, 1)
                    else:
                        V.tensor_tensor(acc[:, i, :], acc[:, i, :], y, ALU.add).then_inc(acc_done, 1)

            F = lambda k: fe[:, k]
            flat = lambda k: fe[:, k].rearrange("p i e -> p (i e)")
            dve.wait_ge(gate_exp, 1)
            then(V.tensor_scalar(flat(1), flat(0), 1.0, None, ALU.add))
            then(V.reciprocal(flat(2), flat(1)))
            then(V.tensor_tensor(F(3), F(2), ebias[:].unsqueeze(1).broadcast_to([P, NT, NE]), ALU.add))
            q4 = flat(3).rearrange("p (g e) -> p g e", e=4)
            G = lambda k: fg[:, k].rearrange("p i g -> p (i g)").unsqueeze(2)
            V.tensor_tensor(G(0), q4[:, :, 0:1], q4[:, :, 1:2], ALU.max)
            V.tensor_tensor(G(1), q4[:, :, 0:1], q4[:, :, 1:2], ALU.min)
            V.tensor_tensor(G(2), q4[:, :, 2:3], q4[:, :, 3:4], ALU.max)
            then(V.tensor_tensor(G(3), q4[:, :, 2:3], q4[:, :, 3:4], ALU.min))
            V.tensor_tensor(G(4), G(0), G(2), ALU.max)
            V.tensor_tensor(G(5), G(0), G(2), ALU.min)
            then(V.tensor_tensor(G(6), G(1), G(3), ALU.max))
            then(V.tensor_tensor(G(5), G(5), G(6), ALU.max))
            then(V.tensor_tensor(G(7), G(4), G(5), ALU.add))

            def ranks(src, n, table, w_, dst, between=(lambda: None, lambda: None)):
                other = src.unsqueeze(2).broadcast_to([P, NT, n, n])
                own = src.unsqueeze(3).broadcast_to([P, NT, n, n])
                V.tensor_tensor(w_[0], other, own, ALU.is_gt)
                then(V.tensor_tensor(w_[1], other, own, ALU.is_equal))
                between[0]()
                m_ = lambda k: w_[k].rearrange("p i a b -> p i (a b)")
                then(V.tensor_tensor(m_(1), m_(1), table.unsqueeze(1).broadcast_to([P, NT, n * n]), ALU.mult))
                then(V.tensor_tensor(m_(1), m_(1), m_(0), ALU.add))
                between[1]()
                then(V.tensor_reduce(dst, w_[1].rearrange("p i a b -> p (i a) b"), AX.X, ALU.add))

            gwv = [gw[:, k].rearrange("p i (a b) -> p i a b", a=4) for k in range(2)]
            ranks(fg[:, 7], NGRP, gbefore[:], gwv, fg[:, 0].rearrange("p i g -> p (i g)"))
            then(V.tensor_scalar(fg[:, 1].rearrange("p i g -> p (i g)"), fg[:, 0].rearrange("p i g -> p (i g)"), float(TOPG), None, ALU.is_lt))
            then(V.tensor_tensor(flat(4).rearrange("p (g e) -> p g e", e=4), q4, G(1).broadcast_to([P, NT * NGRP, 4]), ALU.mult))
            gated(0)
            gated_low(0)

            def second():
                gated(1)
                gated_low(1)
                accumulate(0, range(NT))

            def third():
                gated(2)
                gated_low(2)

            ranks(F(4), NE, before[:], pw, flat(5), (second, third))
            then(V.scalar_tensor_tensor(flat(6), flat(5), float(TOPK), flat(2), ALU.is_lt, ALU.mult))
            then(V.tensor_reduce(hs[:, 0, 0:NT], F(6), AX.X, ALU.add))
            then(V.tensor_scalar(hs[:, 0, 4:4 + NT], hs[:, 0, 0:NT], 1e-20, None, ALU.add))
            then(V.reciprocal(hs[:, 0, 8:8 + NT], hs[:, 0, 4:4 + NT]))
            then(V.tensor_scalar(hs[:, 0, 12:12 + NT], hs[:, 0, 8:8 + NT], 2.5, None, ALU.mult))
            then(V.tensor_tensor(F(7), F(6), hs[:, 0, 12:12 + NT].unsqueeze(2).broadcast_to([P, NT, NE]), ALU.mult))

            accumulate(1, range(NT))
            for e in range(3, NE + 1):
                gated(e)
                accumulate(e - 1, (0, 1))
                gated_low(e)
                accumulate(e - 1, (2, 3))
            accumulate(NE, range(NT))


def kernel(**inputs):
    import concourse.bacc as _bacc
    from concourse.bass_utils import run_bass_kernel_spmd as _run

    f = {k: np.ascontiguousarray(v) for k, v in inputs.items()}
    arrays = {k: f[k] for k in ("x", "ctx_768", "L0_xattn_bo", "L0_attn_b_w2", "L0_attn_gn_weight", "L0_attn_gn_bias", "L0_ffn_e_bias")}
    halves = lambda k, n: f[k].reshape(2, n).T
    twice = lambda k: np.concatenate([f[k], f[k]])[:, None]
    arrays["v_lnx"] = np.ascontiguousarray(np.concatenate([halves("L0_xattn_ln_x_g", HALF), halves("L0_xattn_ln_x_b", HALF)], axis=1))
    arrays["v_cols"] = np.ascontiguousarray(np.concatenate(
        [halves("L0_xattn_ln_l_g", P), halves("L0_xattn_ln_l_b", P), halves("L0_attn_mu0", P), f["L0_attn_bonus"].reshape(P, 1),
         twice("L0_xattn_qn_g"), twice("L0_xattn_kn_g"), f["L0_attn_x_bias"].reshape(5, 2, P).transpose(2, 1, 0).reshape(P, 10)], axis=1))
    for k, src in (("t_Wkv", "L0_xattn_Wkv"), ("t_Wq", "L0_xattn_Wq"), ("t_Wlkv", "L0_xattn_Wlkv"), ("t_Wo", "L0_xattn_Wo"),
                   ("t_W_x0", "L0_attn_W_x0"), ("t_W_x2", "L0_attn_W_x2"), ("t_W_r", "L0_attn_W_r"),
                   ("t_W_k", "L0_attn_W_k"), ("t_W_w1", "L0_attn_W_w1"), ("t_W_w2", "L0_attn_W_w2"), ("t_W_v", "L0_attn_W_v"),
                   ("t_W_g", "L0_attn_W_g"), ("t_W_o", "L0_attn_W_o"), ("t_gate_w", "L0_ffn_gate_w")):
        arrays[k] = np.ascontiguousarray(f[src].T)
    channels = lambda w: w.transpose(0, 2, 1).reshape(len(w), 2, P, INTER).transpose(0, 2, 1, 3).reshape(len(w), P, 2 * INTER)
    with_shared = lambda k: np.concatenate([f["L0_ffn_shared_" + k + "_w"][None], f["L0_ffn_" + k + "_proj"]])
    arrays["p_experts"] = np.ascontiguousarray(np.concatenate(
        [channels(with_shared("gate")), channels(with_shared("up")), with_shared("down").transpose(0, 2, 1)], axis=2))
    mask = f["mask_BxS2_bk0"].astype(np.int32)
    lead = mask[:, 0:FULL * P].reshape(B, P, FULL).transpose(0, 2, 1).reshape(B, FULL * P)
    arrays["p_mask"] = np.ascontiguousarray(np.concatenate([lead, mask[:, FULL * P:], np.ones((B, MROW - S), np.int32)], axis=1).reshape(P, MPIECE))
    arrays.update(constants())

    nc = _bacc.Bacc("TRN2", target_bir_lowering=False, num_devices=1)
    aps = {k: nc.dram_tensor(f"in_{k}", v.shape, mybir.dt.from_np(v.dtype), kind="ExternalInput").ap() for k, v in arrays.items()}
    out = nc.dram_tensor("out_0", (B, T, D), F32, kind="ExternalOutput").ap()
    build(nc, aps, out)
    r = _run(nc, [{f"in_{k}": v for k, v in arrays.items()}], core_ids=[0])
    return r.results[0]["out_0"]
```
